# Optimizing a Trainium2 kernel written in Bass

```python
import numpy as np
import jax
import jax.numpy as jnp

def _softmax(x, axis=-1):
    return jax.nn.softmax(x, axis=axis)

def _gelu(x):
    return jax.nn.gelu(x, approximate=True)

def _silu(x):
    return jax.nn.silu(x)

def _sigmoid(x):
    return jax.nn.sigmoid(x)

def _layernorm(x, axis=-1, eps=1e-05):
    m = jnp.mean(x, axis=axis, keepdims=True)
    v = jnp.var(x, axis=axis, keepdims=True)
    return (x - m) / jnp.sqrt(v + eps)

def _scatter_add(tgt, idx, src, axis=0):
    return tgt.at[idx].add(src)

def _segment_sum(src, seg, n):
    return jax.ops.segment_sum(src, seg, n)
kernel_name = 'mk_xattn_seq_d1_seqx_r4_1aaac0'

def setup_inputs(seed: int=0):
    np.random.seed(seed)
    _w = jnp.asarray

    def _rec_inputs():
        import jax
        import jax.numpy as jnp
        _rk = jax.random.key(seed)
        x = -0.000125 + 0.9999 * jax.random.normal(jax.random.fold_in(_rk, 1), (2, 512, 1024), jnp.float32)
        _lenS = 512 - jax.random.randint(jax.random.fold_in(_rk, 7), (2,), 0, max(1, 512 // 4) + 1, jnp.int32)
        _lenS2 = 1024 - jax.random.randint(jax.random.fold_in(_rk, 8), (2,), 0, max(1, 1024 // 4) + 1, jnp.int32)
        _ctx_4096P = jax.random.normal(jax.random.fold_in(_rk, 11), (2, 16, 1024), jnp.float32)
        _ctx_4096c = jax.random.dirichlet(jax.random.fold_in(_rk, 511), 0.3 * jnp.ones((16,), jnp.float32), (2, 1024))
        _ctx_4096t = jnp.einsum('bsk,bkd->bsd', _ctx_4096c, _ctx_4096P)
        _ctx_4096t = _ctx_4096t * jax.lax.rsqrt(jnp.mean(jnp.square(_ctx_4096t)) + 1e-12) * 0.953939
        ctx_4096 = 0.000227908 + 0.99994 * (_ctx_4096t + 0.3 * jax.random.normal(jax.random.fold_in(_rk, 611), (2, 1024, 1024), jnp.float32))
        _validS = jnp.arange(512)[None, :] < _lenS[:, None]
        _validS2 = jnp.arange(1024)[None, :] < _lenS2[:, None]
        _causal = jnp.tril(jnp.ones((512, 512), dtype=bool))
        mask_BxS2_bf1 = jnp.ones((2, 1024), dtype=bool)
        return (x, ctx_4096, mask_BxS2_bf1)
    x, ctx_4096, mask_BxS2_bf1 = _rec_inputs()

    def _L0_xattn_setup():
        import jax, jax.numpy as jnp
        import numpy as np
        HIDDEN = 1024
        HEADS = 32
        HEAD_DIM = HIDDEN // HEADS
        LN_EPS = 1e-05

        def _split_heads(x):
            B, S, _ = x.shape
            return x.reshape(B, S, HEADS, HEAD_DIM).transpose(0, 2, 1, 3)
        key = jax.random.key(seed)
        ks = jax.random.split(key, 7)
        B, S, SLOTS = (2, 1024, 128)
        hidden_states = jax.random.normal(ks[0], (B, S, HIDDEN), dtype=jnp.float32)
        memory_keys = jax.random.normal(ks[1], (B, SLOTS, HIDDEN), dtype=jnp.float32)
        memory_values = jax.random.normal(ks[2], (B, SLOTS, HIDDEN), dtype=jnp.float32)
        attention_mask = jnp.ones((B, SLOTS), dtype=jnp.bool_)
        Wq = jax.random.normal(ks[3], (HIDDEN, HIDDEN), dtype=jnp.float32) / np.sqrt(HIDDEN)
        Wout = jax.random.normal(ks[4], (HIDDEN, HIDDEN), dtype=jnp.float32) / np.sqrt(HIDDEN)
        ln_gamma = jnp.ones((HIDDEN,), dtype=jnp.float32)
        ln_beta = jnp.zeros((HIDDEN,), dtype=jnp.float32)
        return dict(hidden_states=hidden_states, memory_keys=memory_keys, memory_values=memory_values, attention_mask=attention_mask, Wq=Wq, Wout=Wout, ln_gamma=ln_gamma, ln_beta=ln_beta)
    _L0_xattn_all = _L0_xattn_setup()
    _L0_xattn_in = {k: v for k, v in _L0_xattn_all.items() if k in ('Wq', 'Wout', 'ln_gamma', 'ln_beta')}
    del _L0_xattn_all
    return {'x': x, 'ctx_4096': ctx_4096, 'mask_BxS2_bf1': mask_BxS2_bf1, 'L0_xattn_Wq': _L0_xattn_in['Wq'], 'L0_xattn_Wout': _L0_xattn_in['Wout'], 'L0_xattn_ln_gamma': _L0_xattn_in['ln_gamma'], 'L0_xattn_ln_beta': _L0_xattn_in['ln_beta']}

def reference(x, ctx_4096, mask_BxS2_bf1, L0_xattn_Wq, L0_xattn_Wout, L0_xattn_ln_gamma, L0_xattn_ln_beta):
    import jax
    import jax.numpy as jnp

    def _L0_xattn_ref(hidden_states, memory_keys, memory_values, attention_mask, Wq, Wout, ln_gamma, ln_beta):
        import jax, jax.numpy as jnp
        import numpy as np
        HIDDEN = 1024
        HEADS = 32
        HEAD_DIM = HIDDEN // HEADS
        LN_EPS = 1e-05

        def _split_heads(x):
            B, S, _ = x.shape
            return x.reshape(B, S, HEADS, HEAD_DIM).transpose(0, 2, 1, 3)
        residual = hidden_states
        mu = jnp.mean(hidden_states, axis=-1, keepdims=True)
        var = jnp.var(hidden_states, axis=-1, keepdims=True)
        x = (hidden_states - mu) * jax.lax.rsqrt(var + LN_EPS) * ln_gamma + ln_beta
        Q = _split_heads(x @ Wq.T)
        K = _split_heads(memory_keys)
        V = _split_heads(memory_values)
        scale = HEAD_DIM ** (-0.5)
        scores = jnp.einsum('bhsd,bhtd->bhst', Q, K) * scale
        mask = attention_mask[:, None, None, :]
        scores = jnp.where(mask, scores, -jnp.inf)
        probs = jax.nn.softmax(scores, axis=-1)
        attn = jnp.einsum('bhst,bhtd->bhsd', probs, V)
        B, _, S, _ = attn.shape
        attn = attn.transpose(0, 2, 1, 3).reshape(B, S, HIDDEN)
        out = attn @ Wout.T
        return residual + out
    x = _L0_xattn_ref(x, ctx_4096, ctx_4096, mask_BxS2_bf1, L0_xattn_Wq, L0_xattn_Wout, L0_xattn_ln_gamma, L0_xattn_ln_beta)
    return x

_drawn_inputs = setup_inputs


def setup_inputs(seed=0):
    import zlib

    import numpy as np

    out = dict(_drawn_inputs(seed))
    spreads = {'L0_xattn_ln_gamma': (1.0, 0.2), 'L0_xattn_ln_beta': (0.0, 0.364)}
    factors = {}
    for name, (base, spread) in spreads.items():
        noise = np.random.default_rng([zlib.crc32(name.encode()), seed]).standard_normal(out[name].shape)
        drawn = base * np.exp(spread * noise) if base else spread * noise
        out[name] = jnp.asarray(drawn.astype(out[name].dtype))
    for name, factor in factors.items():
        out[name] = (out[name] * factor).astype(out[name].dtype)
    return out
```

```python
import numpy as np
import concourse.bass as bass
from concourse import mybir

F32 = mybir.dt.float32
F32R = mybir.dt.float32r
BF16 = mybir.dt.bfloat16
U8 = mybir.dt.uint8
ALU = mybir.AluOpType
ACT = mybir.ActivationFunctionType

BATCH, S, HID = 2, 512, 1024
T = 1024
HD = 32
P = 128
HPG = P // HD
GROUPS = HID // P
STEPS = GROUPS * BATCH
TOK = BATCH * S
TOK_TILES = TOK // P
KCH = HID // P
TT = T // P
ST = S // P
RING = 4
BIAS = 3 * HD
ROWS = BIAS + 2
SCALE = float(HD) ** -0.5
EPS = 1e-5
BIG = 3.0e38
POOL_TILES = (0, 1, 3, 4, 6)
ADDS = len(POOL_TILES) - 1
SUM_SLOT = 1

M_ITEMS = HPG * ST
EARLY = M_ITEMS // 2


def step_items(last2, last1):
    order = [("keys", 2, 0)] + [("max", 1, i) for i in range(EARLY, M_ITEMS)]
    order += [("max", 2, i) for i in range(3)]
    slots = [order[2 * s:2 * s + 2] for s in range(6)]
    slots.append([("bias", 1, 0), ("max", 2, 3), ("max", 2, 4)])
    slots.append([("max", 2, 5), ("max", 2, 6), ("max", 2, 7)])
    gone = {2} if last2 else set()
    gone |= {1, 2} if last1 else set()
    return [[i for i in s if i[1] not in gone] for s in slots]


def items_of(n):
    return step_items(n + 2 >= STEPS, n + 1 >= STEPS)


HEAD, REST = range(0, 3), range(3, TT)

PRO_VECTOR_ITEMS = 2 + M_ITEMS + EARLY
STEP_VECTOR_ITEMS = 1 + M_ITEMS


def build(nc, x, ctx, mask, wq, wout, gamma, beta, out):
    def sb(name, shape, dt):
        return nc.alloc_sbuf_tensor(name, shape, dt)

    ident = sb("ident", [P, P], F32)
    ones = sb("ones", [P, HD], F32)
    QA = sb("QA", [P, STEPS, S], F32)
    R = sb("R", [P, RING * HPG * (T + S)], F32R)
    KSZ, QSZ = HPG * T, HPG * S
    KS = [R[:, r * KSZ:(r + 1) * KSZ].rearrange("p (h t) -> p h t", h=HPG) for r in range(RING)]
    q0 = RING * KSZ
    QS = [R[:, q0 + r * QSZ:q0 + (r + 1) * QSZ].rearrange("p (h s) -> p h s", h=HPG) for r in range(RING)]
    XTh = R[:, 0:KCH * TOK].rearrange("p (k s) -> p k s", k=KCH)
    XTl = R[:, KCH * TOK:2 * KCH * TOK].rearrange("p (k s) -> p k s", k=KCH)
    w0 = 2 * KCH * TOK
    WTh = [R[:, w0 + g * HID:w0 + (g + 1) * HID].rearrange("p (k n) -> p k n", k=KCH) for g in range(2)]
    WTl = [R[:, w0 + (2 + g) * HID:w0 + (3 + g) * HID].rearrange("p (k n) -> p k n", k=KCH) for g in range(2)]
    WOh, WOl = XTh, XTl
    AH, AL = WTh, WTl
    C = [sb(f"C{r}", [P, TT, P], F32) for r in range(RING)]
    YT = [C[3][:, 4 * i:4 * i + 4, :].rearrange("p a c -> p (a c)") for i in range(2)]
    PR = sb("PR", [P, RING, HPG, S], F32)
    XS = PR[:, :, :, :].rearrange("p a b c -> p (a b c)").rearrange("p (t c) -> p t c", t=TOK_TILES)
    acc = sb("acc", [P, HPG, S], F32)
    WS = [acc[:, 2 * g:2 * g + 2, :].rearrange("p a b -> p (a b)") for g in range(2)]
    KTh = sb("KTh", [P, T], F32R)
    KTl = sb("KTl", [P, T], F32R)
    QTh = sb("QTh", [P, S], F32R)
    QTl = sb("QTl", [P, S], F32R)
    rsum = sb("rsum", [P, S], F32)
    BT = sb("BT", [2 * HPG, S], F32R)
    maskadd = sb("maskadd", [P, BATCH, T], BF16)
    maskrow = rsum[:, :].bitcast(U8).rearrange("p (b t) -> p b t", b=BATCH)
    mx = sb("mx", [P, 2, M_ITEMS], F32)
    mxh = sb("mxh", [P, 2, M_ITEMS], F32R)
    MM = sb("MM", [P, (ST - 1) * 2 * HPG + P], F32)
    aux = sb("aux", [P, P], F32)
    auxm = sb("auxm", [P, P], U8)
    cols = sb("cols", [P, P], F32)
    stats = sb("stats", [P, TOK_TILES, 2, 6], F32)
    mv = sb("mv", [P, TOK_TILES, 2], F32)
    veps = sb("veps", [P, TOK_TILES], F32)
    sd = sb("sd", [P, TOK_TILES], F32)
    rstd = sb("rstd", [P, TOK_TILES], F32)
    newt = sb("newt", [P, TOK_TILES], F32)
    nmr = sb("nmr", [P, TOK_TILES], F32)
    GAM, BET, MSK = 0, 32, 64

    MX = [nc.alloc_psum_tensor(f"MX{i}", [P, T], F32) for i in range(2)]
    SX = [nc.alloc_psum_tensor(f"SX{i}", [P, S], F32) for i in range(2)]
    PV = nc.alloc_psum_tensor("PV", [P, S], F32)
    SM = nc.alloc_psum_tensor("SM", [P, S], F32)
    QP = [PV, SM]

    sem = nc.alloc_semaphore
    const_done = sem("const_done")
    aux_in, aux_ready, aux_t, cols_ready = sem("aux_in"), sem("aux_ready"), sem("aux_t"), sem("cols_ready")
    maskrow_in, mask_ready = sem("maskrow_in"), sem("mask_ready")
    onesrow_ready, onesrow_in = sem("onesrow_ready"), sem("onesrow_in")
    x_in = [sem(f"x_in{t}") for t in range(TOK_TILES)]
    chain = sem("chain")
    var_ready, sd_ready, norm_ready, xn_ready = sem("var_ready"), sem("sd_ready"), sem("norm_ready"), sem("xn_ready")
    xt_ready, y_ready, xt_split = sem("xt_ready"), sem("y_ready"), sem("xt_split")
    w_in = [sem(f"w_in{g}") for g in range(2)]
    wt_ready, wt_hi, wt_lo, q_done, q_copied = sem("wt_ready"), sem("wt_hi"), sem("wt_lo"), sem("q_done"), sem("q_copied")
    c_in = [sem(f"c_in{r}") for r in range(RING)]
    kt_ready, kt_hi, kt_lo, qt_hi, qt_lo = sem("kt_ready"), sem("kt_hi"), sem("kt_lo"), sem("qt_hi"), sem("qt_lo")
    stack_in = [sem(f"stack_in{h}") for h in range(HPG)]
    m_ready, mx_freed, mm_ready, bt_ready, bt_done, bias_in = (
        sem("m_ready"), sem("mx_freed"), sem("mm_ready"), sem("bt_ready"), sem("bt_done"), sem("bias_in"))
    scores_ready, exp_done, tile_used, pool_used = sem("scores_ready"), sem("exp_done"), sem("tile_used"), sem("pool_used")
    gate = sem("gate")
    pv_done, pv_copied, sums_done, rsum_done, attn_done = (
        sem("pv_done"), sem("pv_copied"), sem("sums_done"), sem("rsum_done"), sem("attn_done"))
    wo_in = [sem(f"wo_in{g}") for g in range(2)]
    wo_ready, wo_hi, wo_lo = sem("wo_ready"), sem("wo_hi"), sem("wo_lo")
    xr_in = [sem(f"xr_in{q}") for q in range(2)]
    ah_done, al_done, o_ready, o_added = sem("ah_done"), sem("al_done"), sem("o_ready"), sem("o_added")
    out_in = [sem(f"out_in{q}") for q in range(2)]

    ctx_v = ctx.rearrange("b (t p) (g c) -> p b t g c", p=P, c=P)
    xt_v = x.rearrange("b (t p) c -> p (b t) c", p=P)
    out_v = out.rearrange("b (t p) c -> p (b t) c", p=P)
    wq_v = wq.rearrange("(g p) c -> p g c", p=P)
    wo_v = wout.rearrange("(g p) c -> p g c", p=P)
    QAt = QA[:, :, :].rearrange("p (g b) s -> p g (b s)", b=BATCH)

    main_loops = STEPS // RING

    with nc.Block() as block:

        @block.sync
        def _(sp):
            for t in range(4):
                sp.dma_start(XS[:, t, :], xt_v[:, t, :]).then_inc(x_in[t], 16)
            sp.dma_start(WS[0], wq_v[:, 0, :]).then_inc(w_in[0], 16)
            sp.dma_start(WS[1], wq_v[:, 1, :]).then_inc(w_in[1], 16)
            for t in range(4, TOK_TILES):
                sp.dma_start(XS[:, t, :], xt_v[:, t, :]).then_inc(x_in[t], 16)
            for n in range(3):
                sp.dma_start(C[n][:, :, :], ctx_v[:, n % BATCH, :, n // BATCH, :]).then_inc(c_in[n], 16)
            with sp.Fori(0, GROUPS // 2 - 1) as i:
                for g in range(2):
                    sp.wait_ge(wt_ready, 2 * i + g + 1)
                    sp.dma_start(WS[g], wq_v[:, bass.ds(2 * i + g + 2, 1), :].rearrange("p a c -> p (a c)")).then_inc(w_in[g], 16)

            def stack(n, u):
                r = u % RING
                sp.wait_ge(qt_hi, n + 1)
                sp.wait_ge(kt_hi, n + 1)
                sp.wait_ge(kt_lo, n + 1)
                sp.wait_ge(qt_lo, n + 1)
                for h in range(HPG):
                    own = slice(h * HD, (h + 1) * HD)
                    sp.dma_start(KS[r][0:HD, h, :].bitcast(F32), KTh[own, :].bitcast(F32)).then_inc(stack_in[h], 16)
                    sp.dma_start(KS[r][HD:2 * HD, h, :].bitcast(F32), KTl[own, :].bitcast(F32)).then_inc(stack_in[h], 16)
                    sp.dma_start(KS[r][2 * HD:3 * HD, h, :].bitcast(F32), KTh[own, :].bitcast(F32)).then_inc(stack_in[h], 16)
                    sp.dma_start(QS[r][0:HD, h, :].bitcast(F32), QTh[own, :].bitcast(F32)).then_inc(stack_in[h], 16)
                    sp.dma_start(QS[r][HD:2 * HD, h, :].bitcast(F32), QTh[own, :].bitcast(F32)).then_inc(stack_in[h], 16)
                    sp.dma_start(QS[r][2 * HD:3 * HD, h, :].bitcast(F32), QTl[own, :].bitcast(F32)).then_inc(stack_in[h], 16)

            def bias_rows(n, u):
                r = u % RING
                sp.wait_ge(bt_done, n + 1)
                for h in range(HPG):
                    sp.dma_start(QS[r][BIAS:ROWS, h, :].bitcast(F32), BT[2 * h:2 * h + 2, :].bitcast(F32)).then_inc(bias_in, 16)

            sp.wait_ge(q_done, 1 + BATCH * GROUPS)
            sp.wait_ge(onesrow_ready, 1)
            for r in range(RING):
                sp.dma_start(KS[r][BIAS:ROWS, :, :].rearrange("p h t -> p (h t)").bitcast(F32),
                             PR[0:2, 0:2, :, :].rearrange("p a b c -> p (a b c)")).then_inc(onesrow_in, 16)
            stack(0, 0)
            stack(1, 1)
            bias_rows(0, 0)

            def step(j, u, last):
                n = RING * j + u
                if not (last and u >= 1):
                    sp.wait_ge(pv_done, 1 + n)
                    m = u + 3
                    sp.dma_start(C[m % RING][:, :, :],
                                 ctx_v[:, m % BATCH, :, bass.ds(2 * j + m // BATCH, 1), :].rearrange("p t a c -> p t (a c)")
                                 ).then_inc(c_in[m % RING], 16)
                if not (last and u >= 2):
                    stack(n + 2, u + 2)
                if not (last and u >= 3):
                    bias_rows(n + 1, u + 1)

            with sp.Fori(0, main_loops - 1) as j:
                for u in range(RING):
                    step(j, u, False)
            for u in range(RING):
                step(main_loops - 1, u, True)
            sp.wait_ge(sums_done, STEPS)
            for g in range(2):
                sp.dma_start(WS[g], wo_v[:, g, :]).then_inc(wo_in[g], 16)
            for q in range(2):
                sp.dma_start(XS[:, q, :], xt_v[:, q, :]).then_inc(xr_in[q], 16)
            with sp.Fori(0, GROUPS // 2 - 1) as i:
                for g in range(2):
                    sp.wait_ge(wo_ready, 2 * i + g + 1)
                    sp.dma_start(WS[g], wo_v[:, bass.ds(2 * i + g + 2, 1), :].rearrange("p a c -> p (a c)")).then_inc(wo_in[g], 16)

            def store(t, q):
                sp.wait_ge(o_added, 2 * t + 2)
                sp.dma_start(out_v[:, bass.ds(t, 1), :].rearrange("p a c -> p (a c)"), XS[:, 2 + q, :]).then_inc(out_in[q], 16)

            with sp.Fori(0, TOK_TILES // 2 - 1) as i:
                for q in range(2):
                    t = 2 * i + q
                    store(t, q)
                    sp.dma_start(XS[:, q, :], xt_v[:, bass.ds(t + 2, 1), :].rearrange("p a c -> p (a c)")).then_inc(xr_in[q], 16)
            for q in range(2):
                store(TOK_TILES - 2 + q, q)
            for q in range(2):
                sp.wait_ge(out_in[q], 16 * TOK_TILES // 2)

        @block.gpsimd
        def _(pool):
            pool.sem_inc(attn_done, 1)
            nc.gpsimd.memset(ident[:, :], 0.0).then_inc(const_done, 1)
            nc.gpsimd.memset(aux[:, :], 0.0).then_inc(const_done, 1)
            nc.gpsimd.memset(ones[:, :], 1.0).then_inc(const_done, 1)
            pool.wait_ge(const_done, 3)
            nc.gpsimd.affine_select(out=ident[:, :], in_=ident[:, :], compare_op=ALU.not_equal, fill=1.0,
                                    base=0, pattern=[[-1, P]], channel_multiplier=1).then_inc(const_done, 1)
            pool.dma_start(aux[GAM:GAM + KCH, :], gamma.rearrange("(k p) -> k p", p=P)).then_inc(aux_in, 16)
            pool.dma_start(aux[BET:BET + KCH, :], beta.rearrange("(k p) -> k p", p=P)).then_inc(aux_in, 16)
            pool.dma_start(auxm[MSK:MSK + BATCH * TT, :], mask.rearrange("b (t p) -> (b t) p", p=P)).then_inc(aux_in, 16)
            pool.dma_start(maskrow, mask.rearrange("b t -> (b t)").partition_broadcast(P).rearrange("p (b t) -> p b t", b=BATCH)).then_inc(maskrow_in, 16)
            nc.gpsimd.memset(MM[:, :], 0.0).then_inc(const_done, 1)
            pool.wait_ge(xt_ready, BATCH * KCH)
            nc.gpsimd.memset(PR[0:2, 0:2, :, :], 1.0).then_inc(onesrow_ready, 1)

            def query_low(n):
                pool.wait_ge(qt_hi, n + 1)
                pool.sem_inc(gate, 1)
                nc.gpsimd.tensor_tensor(QTl[:, :], QA[:, bass.ds(n, 1), :].rearrange("p a s -> p (a s)"),
                                        QTh[:, :].bitcast(F32), ALU.subtract).then_inc(qt_lo, 1)

            pool.wait_ge(q_copied, 2 + BATCH * GROUPS)
            query_low(0)
            query_low(1)
            pool.sem_inc(pool_used, ADDS)

            def normalise(n):
                pool.wait_ge(pv_copied, n + 1)
                pool.wait_ge(rsum_done, 1 + 4 * (n + 1))
                pool.sem_inc(gate, 1)
                at = QA[:, bass.ds(n, 1), :].rearrange("p a s -> p (a s)")
                nc.gpsimd.tensor_tensor(at, at, rsum[:, :], ALU.mult).then_inc(attn_done, 1)

            def add_probs(n, k):
                first, tt = POOL_TILES[0], POOL_TILES[k + 1]
                if k == 0:
                    pool.wait_ge(sums_done, n)
                else:
                    pool.wait_ge(pool_used, ADDS * n + ADDS + k)
                pool.wait_ge(exp_done, 2 + TT * HPG * n + HPG * (tt + 1))
                a = PR[:, first % RING, :, :] if k == 0 else acc[:, :, :]
                nc.gpsimd.tensor_tensor(acc[:, :, :], a, PR[:, tt % RING, :, :], ALU.add).then_inc(pool_used, 1)

            def step(j, u, last):
                n = RING * j + u
                for k in range(1, ADDS):
                    add_probs(n, k)
                if not (last and u >= 1):
                    query_low(n + 3)
                if not (last and u >= 3):
                    add_probs(n + 1, 0)
                normalise(n)

            query_low(2)
            add_probs(0, 0)
            with pool.Fori(0, main_loops - 1) as j:
                for u in range(RING):
                    step(j, u, False)
            for u in range(RING):
                step(main_loops - 1, u, True)

        @block.scalar
        def _(act):
            for b in range(BATCH):
                act.wait_ge(var_ready, b + 1)
                ts = slice(b * ST, (b + 1) * ST)
                nc.scalar.activation(sd[:, ts], veps[:, ts], ACT.Sqrt).then_inc(sd_ready, 1)
                act.wait_ge(norm_ready, b + 1)
                for t in range(b * ST, (b + 1) * ST):
                    nc.scalar.activation(XS[:, t, :], XS[:, t, :], ACT.Identity, scale=rstd[:, t:t + 1],
                                         bias=nmr[:, t:t + 1]).then_inc(xn_ready, 1)
                if b == 0:
                    act.wait_ge(cols_ready, 1)
                for k in range(KCH):
                    i = b * KCH + k
                    act.wait_ge(xt_ready, i + 1)
                    if i >= 2:
                        act.wait_ge(xt_split, i - 1)
                    nc.scalar.activation(YT[i % 2], SX[i % 2][:, :], ACT.Identity, scale=cols[:, GAM + k:GAM + k + 1],
                                         bias=cols[:, BET + k:BET + k + 1]).then_inc(y_ready, 1)

            def wt_high(g, par):
                act.wait_ge(wt_ready, g + 1)
                nc.scalar.activation(WTh[par].rearrange("p k n -> p (k n)"), MX[par][:, :], ACT.Copy).then_inc(wt_hi, 1)

            def q_copy(g):
                for b in range(BATCH):
                    act.wait_ge(q_done, 1 + 2 * g + b + 1)
                    nc.scalar.activation(QA[:, bass.ds(BATCH * g + b, 1), :].rearrange("p a s -> p (a s)"),
                                         QP[b][:, :], ACT.Copy).then_inc(q_copied, 1)

            act.sem_inc(q_copied, 2)
            wt_high(0, 0)

            def q_group(g, par, more):
                if more:
                    act.wait_ge(q_done, 1 + 2 * g)
                    wt_high(g + 1, 1 - par)
                q_copy(g)

            with act.Fori(0, GROUPS // 2 - 1) as i:
                for par in range(2):
                    q_group(2 * i + par, par, True)
            q_group(GROUPS - 2, 0, True)
            q_group(GROUPS - 1, 1, False)

            def key_high(n, par):
                act.wait_ge(kt_ready, n + 1)
                for h in range(HPG):
                    act.wait_ge(stack_in[h], 96 * n)
                nc.scalar.activation(KTh[:, :], MX[par][:, :], ACT.Copy).then_inc(kt_hi, 1)

            def bias_copy(n, par):
                act.wait_ge(bt_ready, n + 1)
                act.wait_ge(bias_in, 64 * n)
                nc.scalar.activation(BT[:, :], MX[par][0:2 * HPG, 0:S], ACT.Copy).then_inc(bt_done, 1)

            def exps(n, u, tt, pair):
                for h in (2 * pair, 2 * pair + 1):
                    q = TT * HPG * n + HPG * tt + h
                    if h == 0:
                        act.wait_ge(tile_used, TT * n + tt + 1)
                        old, m = (tt - RING, n) if tt >= RING else (tt + RING, n - 1)
                        if old in POOL_TILES:
                            act.wait_ge(pool_used, ADDS * m + ADDS + max(POOL_TILES.index(old), 1))
                    act.wait_ge(scores_ready, q + 1)
                    b = u % BATCH
                    nc.scalar.activation(PR[:, tt % RING, h, :], SX[h % 2][:, :], ACT.Exp, scale=SCALE,
                                         bias=cols[:, MSK + b * TT + tt:MSK + b * TT + tt + 1]).then_inc(exp_done, 1)

            key_high(0, 0)
            key_high(1, 1)
            act.sem_inc(exp_done, 2)
            bias_copy(0, 0)

            def pv_copy(n):
                act.wait_ge(pv_done, 1 + n + 1)
                nc.scalar.activation(QA[:, bass.ds(n, 1), :].rearrange("p a s -> p (a s)"), PV[:, :], ACT.Copy).then_inc(pv_copied, 1)

            def slots(n, u, items, which, first=False):
                at = 1 + sum(len(i) for i in items[:which[0]])
                for tt in which:
                    exps(n, u, tt, 0)
                    for kind, a, i in items[tt]:
                        if kind == "keys":
                            key_high(n + a, at % 2)
                        if kind == "bias":
                            bias_copy(n + a, at % 2)
                        at += 1
                    exps(n, u, tt, 1)
                    if tt == 0 and not first:
                        pv_copy(n - 1)

            slots(0, 0, step_items(False, False), HEAD, first=True)
            with act.Fori(0, main_loops - 1) as j:
                for u in range(RING):
                    slots(RING * j + u, u, step_items(False, False), REST)
                    slots(RING * j + u + 1, u + 1, step_items(False, False), HEAD)
            for n in range(STEPS - RING, STEPS):
                slots(n, n % RING, items_of(n), REST)
                if n < STEPS - 1:
                    slots(n + 1, (n + 1) % RING, items_of(n + 1), HEAD)
            pv_copy(STEPS - 1)

            with act.Fori(0, GROUPS // 2) as i:
                for par in range(2):
                    o = 2 * i + par
                    act.wait_ge(wo_ready, o + 1)
                    nc.scalar.activation(WOh[:, :, bass.ds(o * P, P)], MX[par][:, :].rearrange("p (g n) -> p g n", n=P),
                                         ACT.Copy).then_inc(wo_hi, 1)

        @block.vector
        def _(dve):
            links = [0]
            dve.sem_inc(wt_lo, 1)
            dve.sem_inc(rsum_done, 1)

            def link(ins):
                links[0] += 1
                ins.then_inc(chain, 1)
                dve.wait_ge(chain, links[0])

            for b in range(BATCH):
                ts = slice(b * ST, (b + 1) * ST)
                for t in range(b * ST, (b + 1) * ST):
                    dve.wait_ge(x_in[t], 16)
                    for half in range(2):
                        ins = nc.vector.bn_stats(stats[:, t, half, :], XS[:, t, half * 512:(half + 1) * 512])
                link(ins)
                for t in range(b * ST, (b + 1) * ST):
                    ins = nc.vector.bn_aggr(mv[:, t, :], stats[:, t, :, :].rearrange("p a b -> p (a b)"))
                link(ins)
                nc.vector.tensor_scalar(veps[:, ts], mv[:, ts, 1], EPS, None, ALU.add).then_inc(var_ready, 1)
                if b == 0:
                    dve.wait_ge(aux_in, 48)
                    dve.wait_ge(const_done, 5)
                    nc.vector.tensor_scalar(aux[MSK:MSK + BATCH * TT, :], auxm[MSK:MSK + BATCH * TT, :], BIG, -BIG,
                                            ALU.mult, ALU.add).then_inc(aux_ready, 1)
                    dve.wait_ge(aux_t, 1)
                    nc.vector.tensor_copy(cols[:, :], MX[1][:, 0:P]).then_inc(cols_ready, 1)
                dve.wait_ge(sd_ready, b + 1)
                link(nc.vector.reciprocal(rstd[:, ts], sd[:, ts]))
                link(nc.vector.tensor_tensor(newt[:, ts], rstd[:, ts], rstd[:, ts], ALU.mult))
                link(nc.vector.tensor_tensor(newt[:, ts], newt[:, ts], veps[:, ts], ALU.mult))
                link(nc.vector.tensor_scalar(newt[:, ts], newt[:, ts], -0.5, 1.5, ALU.mult, ALU.add))
                link(nc.vector.tensor_tensor(rstd[:, ts], rstd[:, ts], newt[:, ts], ALU.mult))
                nc.vector.scalar_tensor_tensor(nmr[:, ts], mv[:, ts, 0], -1.0, rstd[:, ts], ALU.mult, ALU.mult).then_inc(norm_ready, 1)
                for k in range(KCH):
                    i = b * KCH + k
                    dst = slice(b * S, (b + 1) * S)
                    dve.wait_ge(y_ready, i + 1)
                    link(nc.vector.tensor_copy(XTh[:, k, dst], YT[i % 2]))
                    nc.vector.tensor_tensor(XTl[:, k, dst], YT[i % 2], XTh[:, k, dst].bitcast(F32), ALU.subtract).then_inc(xt_split, 1)

            def w_low(g, par):
                dve.wait_ge(wt_hi, g + 1)
                nc.vector.tensor_tensor(WTl[par].rearrange("p k n -> p (k n)"), MX[par][:, :],
                                        WTh[par].rearrange("p k n -> p (k n)").bitcast(F32), ALU.subtract).then_inc(wt_lo, 1)

            w_low(0, 0)
            with dve.Fori(0, GROUPS // 2 - 1) as i:
                for par in range(2):
                    w_low(2 * i + par + 1, 1 - par)
            w_low(GROUPS - 1, 1)
            for b in range(BATCH):
                dve.wait_ge(maskrow_in, 16)
                ins = nc.vector.tensor_scalar(maskadd[:, b, :], maskrow[:, b, :], BIG, -BIG, ALU.mult, ALU.add)
            link(ins)

            def query_high(n):
                for h in range(HPG):
                    dve.wait_ge(stack_in[h], 96 * n)
                nc.vector.tensor_copy(QTh[:, :], QA[:, bass.ds(n, 1), :].rearrange("p a s -> p (a s)")).then_inc(qt_hi, 1)

            def key_low(n, par):
                dve.wait_ge(kt_hi, n + 1)
                nc.vector.tensor_tensor(KTl[:, :], MX[par][:, :], KTh[:, :].bitcast(F32), ALU.subtract).then_inc(kt_lo, 1)
                dve.wait_ge(kt_lo, n + 1)
                dve.sem_inc(mx_freed, 1)

            def maximum(n, u, i, par):
                h, st = divmod(i, ST)
                c = st * HPG + h
                dve.wait_ge(m_ready, M_ITEMS * n + i + 1)
                dve.sem_inc(gate, 1)
                nc.vector.tensor_tensor_reduce(out=MX[par][:, :], in0=MX[par][:, :], in1=maskadd[:, u % BATCH, :], scale=1.0,
                                               scalar=-BIG, op0=ALU.add, op1=ALU.max,
                                               accum_out=mx[:, u % 2, c:c + 1]).then_inc(mx_freed, 1)

            def bias_columns(n, u, freed):
                dve.wait_ge(mx_freed, freed)
                dve.wait_ge(bt_ready, n)
                nc.vector.tensor_scalar(mxh[:, u % 2, :], mx[:, u % 2, :], -1.0, None, ALU.mult).then_inc(mm_ready, 1)
                dve.wait_ge(mm_ready, 3 * n + 1)
                hi = mxh[:, u % 2, :].bitcast(F32)
                cols_of = MM[:, 0:ST * 2 * HPG].rearrange("p (s h a) -> p s h a", h=HPG, a=2)
                nc.vector.tensor_copy(cols_of[:, :, :, 0], hi.rearrange("p (s h) -> p s h", h=HPG)).then_inc(mm_ready, 1)
                nc.vector.scalar_tensor_tensor(cols_of[:, :, :, 1], mx[:, u % 2, :].rearrange("p (s h) -> p s h", h=HPG), -1.0,
                                               hi.rearrange("p (s h) -> p s h", h=HPG), ALU.mult, ALU.subtract).then_inc(mm_ready, 1)

            def recip(n, piece):
                dve.wait_ge(sums_done, n + 1)
                if piece == 0:
                    dve.wait_ge(attn_done, 1 + n)
                at = slice(piece * P, (piece + 1) * P)
                nc.vector.reciprocal(rsum[:, at], SM[:, at]).then_inc(rsum_done, 1)

            dve.wait_ge(q_copied, 2 + BATCH * GROUPS)
            query_high(0)
            key_low(0, 0)
            query_high(1)
            key_low(1, 1)
            for i in range(M_ITEMS):
                maximum(0, 0, i, i % 2)
            bias_columns(0, 0, 2 + M_ITEMS)
            for i in range(EARLY):
                maximum(1, 1, i, (i + 1) % 2)

            def slots(n, u, items, which, first=False):
                before = [i for slot in items[:which[0]] for i in slot]
                at = 1 + len(before)
                freed = PRO_VECTOR_ITEMS + STEP_VECTOR_ITEMS * n + sum(i[0] != "bias" for i in before)
                pieces = {SUM_SLOT: [0, 1], SUM_SLOT + 1: [2, 3]}
                if which is HEAD and any(i[0] == "keys" for i in items[0]):
                    query_high(n + 2)
                for tt in which:
                    left = [] if first else pieces.get(tt, [])
                    for kind, a, i in items[tt]:
                        if kind == "keys":
                            key_low(n + a, at % 2)
                            freed = freed + 1
                        if kind == "max":
                            maximum(n + a, u + a, i, at % 2)
                            freed = freed + 1
                            if i == M_ITEMS - 1:
                                bias_columns(n + a, u + a, freed)
                        at += 1
                        if left:
                            recip(n - 1, left.pop(0))
                    for piece in left:
                        recip(n - 1, piece)

            slots(0, 0, step_items(False, False), HEAD, first=True)
            with dve.Fori(0, main_loops - 1) as j:
                for u in range(RING):
                    slots(RING * j + u, u, step_items(False, False), REST)
                    slots(RING * j + u + 1, u + 1, step_items(False, False), HEAD)
            for n in range(STEPS - RING, STEPS):
                slots(n, n % RING, items_of(n), REST)
                if n < STEPS - 1:
                    slots(n + 1, (n + 1) % RING, items_of(n + 1), HEAD)
            for piece in range(4):
                recip(STEPS - 1, piece)
            dve.sem_inc(wo_lo, 2)

            with dve.Fori(0, GROUPS // 2) as i:
                for par in range(2):
                    o = 2 * i + par
                    dve.wait_ge(wo_hi, o + 1)
                    nc.vector.tensor_tensor(WOl[:, :, bass.ds(o * P, P)], MX[par][:, :].rearrange("p (g n) -> p g n", n=P),
                                            WOh[:, :, bass.ds(o * P, P)].bitcast(F32), ALU.subtract).then_inc(wo_lo, 1)
            dve.wait_ge(attn_done, 1 + STEPS)

            def split_attn(t, q):
                src = QAt[:, :, bass.ds(t * P, P)]
                nc.vector.tensor_copy(AH[q][:, :, :], src).then_inc(ah_done, 1)
                dve.wait_ge(ah_done, t + 1)
                nc.vector.tensor_tensor(AL[q][:, :, :], src, AH[q][:, :, :].bitcast(F32), ALU.subtract).then_inc(al_done, 1)

            def add_residual(t, i, q, stored=True):
                dve.wait_ge(xr_in[q], 16 * (i + 1))
                if stored:
                    dve.wait_ge(out_in[q], 16 * i)
                for half in range(2):
                    dve.wait_ge(o_ready, 2 * t + half + 1)
                    cs = slice(half * 512, (half + 1) * 512)
                    nc.vector.tensor_tensor(XS[:, 2 + q, cs], XS[:, q, cs], MX[q][:, cs], ALU.add).then_inc(o_added, 1)

            split_attn(0, 0)
            split_attn(1, 1)
            for q in range(2):
                add_residual(q, 0, q, stored=False)
                split_attn(q + 2, q)
            with dve.Fori(1, TOK_TILES // 2 - 1) as i:
                for q in range(2):
                    add_residual(2 * i + q, i, q)
                    split_attn(2 * i + q + 2, q)
            for q in range(2):
                add_residual(TOK_TILES - 2 + q, TOK_TILES // 2 - 1, q)

        @block.tensor
        def _(pe):
            pe.sem_inc(q_done, 1)
            pe.sem_inc(pv_done, 1)
            pe.wait_ge(const_done, 5)
            pe.wait_ge(aux_ready, 1)
            nc.tensor.transpose(MX[1][:, 0:P], aux[:, :], ident[:, :]).then_inc(aux_t, 1)

            def wt_transposes(g, par, rows_in):
                pe.wait_ge(w_in[par], rows_in)
                for k in range(KCH):
                    ins = nc.tensor.transpose(MX[par][:, k * P:(k + 1) * P], WS[par][:, k * P:(k + 1) * P], ident[:, :])
                ins.then_inc(wt_ready, 1)

            wt_transposes(0, 0, 16)
            for b in range(BATCH):
                pe.wait_ge(xn_ready, (b + 1) * ST)
                for k in range(KCH):
                    i = b * KCH + k
                    if i >= 2:
                        pe.wait_ge(y_ready, i - 1)
                    for t in range(ST):
                        ins = nc.tensor.transpose(SX[i % 2][:, t * P:(t + 1) * P], XS[:, b * ST + t, k * P:(k + 1) * P], ident[:, :])
                    ins.then_inc(xt_ready, 1)

            def project(g, par):
                for b in range(BATCH):
                    pe.wait_ge(q_copied, 2 * g + b + 1)
                    toks = slice(b * S, (b + 1) * S)
                    ops = [(WTh, XTh), (WTl, XTh), (WTh, XTl)]
                    for k in range(KCH):
                        for o, (w, v) in enumerate(ops):
                            ins = nc.tensor.matmul(QP[b][:, :], w[par][:, k, :], v[:, k, toks],
                                                   start=(k == 0 and o == 0), stop=(k == KCH - 1 and o == 2))
                    ins.then_inc(q_done, 1)

            pe.wait_ge(cols_ready, 1)
            pe.wait_ge(xt_split, BATCH * KCH)

            def q_group(g, i, par, more):
                if more:
                    pe.wait_ge(wt_lo, 1 + g)
                    wt_transposes(g + 1, 1 - par, 16 * (i + 1 + par))
                pe.wait_ge(wt_lo, 1 + g + 1)
                project(g, par)

            with pe.Fori(0, GROUPS // 2 - 1) as i:
                for par in range(2):
                    q_group(2 * i + par, i, par, True)
            q_group(GROUPS - 2, GROUPS // 2 - 1, 0, True)
            q_group(GROUPS - 1, GROUPS // 2 - 1, 1, False)

            def keys_item(n, u, par, loads):
                pe.wait_ge(c_in[u % RING], 16 * loads)
                for t in range(TT):
                    ins = nc.tensor.transpose(MX[par][:, t * P:(t + 1) * P], C[u % RING][:, t, :], ident[:, :])
                ins.then_inc(kt_ready, 1)

            def max_item(n, u, i, par):
                h, st = divmod(i, ST)
                if st == 0:
                    pe.wait_ge(stack_in[h], 96 * (n + 1))
                for half in range(2):
                    cs = slice(half * 512, (half + 1) * 512)
                    ins = nc.tensor.matmul(MX[par][:, cs], QS[u % RING][0:BIAS, h, st * P:(st + 1) * P],
                                           KS[u % RING][0:BIAS, h, cs], start=True, stop=True)
                ins.then_inc(m_ready, 1)

            def bias_item(n, par):
                pe.wait_ge(mm_ready, 3 * (n + 1))
                for st in range(ST):
                    ins = nc.tensor.transpose(MX[par][:, st * P:(st + 1) * P], MM[:, st * 2 * HPG:st * 2 * HPG + P], ident[:, :])
                ins.then_inc(bt_ready, 1)

            def scores(n, u, tt, h):
                q = TT * HPG * n + HPG * tt + h
                pe.wait_ge(exp_done, q + 1)
                nc.tensor.matmul(SX[h % 2][:, :], KS[u % RING][0:ROWS, h, tt * P:(tt + 1) * P], QS[u % RING][0:ROWS, h, :],
                                 start=True, stop=True).then_inc(scores_ready, 1)

            def sum_probs(tile, start, stop):
                for h in range(HPG):
                    ins = nc.tensor.matmul(SM[h * HD:(h + 1) * HD, :], ones[:, :], tile(h), start=start, stop=stop,
                                           skip_group_check=True)
                return ins

            def values(n, u, tt):
                pe.wait_ge(exp_done, 2 + TT * HPG * n + HPG * (tt + 1))
                if tt == 0:
                    pe.wait_ge(pv_copied, n)
                for h in range(HPG):
                    ins = nc.tensor.matmul(PV[h * HD:(h + 1) * HD, :], C[u % RING][:, tt, h * HD:(h + 1) * HD],
                                           PR[:, tt % RING, h, :], start=(tt == 0), stop=(tt == TT - 1), skip_group_check=True)
                if tt == TT - 1:
                    ins.then_inc(pv_done, 1)
                if tt in POOL_TILES:
                    ins.then_inc(tile_used, 1)

            def direct_sum(n, tt):
                if tt not in POOL_TILES:
                    if tt == min(set(range(TT)) - set(POOL_TILES)):
                        pe.wait_ge(rsum_done, 1 + 4 * n)
                        ins = sum_probs(lambda h: PR[:, tt % RING, h, :], True, False)
                    else:
                        ins = sum_probs(lambda h: PR[:, tt % RING, h, :], False, False)
                    ins.then_inc(tile_used, 1)

            def last_sum(n):
                pe.wait_ge(pool_used, ADDS * n + 2 * ADDS)
                sum_probs(lambda h: acc[:, h, :], False, True).then_inc(sums_done, 1)

            pe.wait_ge(q_copied, 2 + BATCH * GROUPS)
            keys_item(0, 0, 0, 1)
            keys_item(1, 1, 1, 1)
            for i in range(M_ITEMS):
                pe.wait_ge(mx_freed, i + 1)
                max_item(0, 0, i, i % 2)
            pe.wait_ge(mx_freed, M_ITEMS + 1)
            bias_item(0, 0)
            for i in range(EARLY):
                if i == 1:
                    pe.wait_ge(bt_done, 1)
                else:
                    pe.wait_ge(mx_freed, M_ITEMS + 2 if i == 0 else M_ITEMS + 1 + i)
                max_item(1, 1, i, (i + 1) % 2)
            pe.sem_inc(tile_used, RING)
            pe.wait_ge(onesrow_in, 16 * RING)

            def slots(n, u, loads, items, which, first=False):
                before = [i for slot in items[:which[0]] for i in slot]
                freed = PRO_VECTOR_ITEMS + STEP_VECTOR_ITEMS * n + sum(i[0] != "bias" for i in before)
                kinds = ["max", "max"] + [i[0] for i in before]

                def mx_item(kind, a, i, freed):
                    if kinds[-2] == "bias":
                        pe.wait_ge(bt_done, n + 2)
                    else:
                        pe.wait_ge(mx_freed, freed - (1 if kinds[-1] != "bias" else 0))
                    par = (len(kinds) - 1) % 2
                    if kind == "keys":
                        keys_item(n + a, u + a, par, loads)
                    elif kind == "bias":
                        bias_item(n + a, par)
                    else:
                        max_item(n + a, u + a, i, par)
                    kinds.append(kind)
                    return freed + (kind != "bias")

                if which is HEAD:
                    pe.wait_ge(bias_in, 64 * (n + 1))
                for tt in which:
                    scores(n, u, tt, 0)
                    for it in items[tt][:1]:
                        freed = mx_item(*it, freed)
                    scores(n, u, tt, 1)
                    if tt >= 1:
                        values(n, u, tt - 1)
                    elif not first:
                        values(n - 1, u + RING - 1, TT - 1)
                    scores(n, u, tt, 2)
                    for it in items[tt][1:]:
                        freed = mx_item(*it, freed)
                    scores(n, u, tt, 3)
                    if tt >= 1:
                        direct_sum(n, tt - 1)
                    elif not first:
                        direct_sum(n - 1, TT - 1)
                    if tt == SUM_SLOT and not first:
                        last_sum(n - 1)

            slots(0, 0, 1, step_items(False, False), HEAD, first=True)
            with pe.Fori(0, main_loops - 1) as j:
                for u in range(RING):
                    slots(RING * j + u, u, None, step_items(False, False), REST)
                    slots(RING * j + u + 1, u + 1, j + 1 + (u + 3) // RING, step_items(False, False), HEAD)
            for n in range(STEPS - RING, STEPS):
                slots(n, n % RING, None, items_of(n), REST)
                if n < STEPS - 1:
                    slots(n + 1, (n + 1) % RING, (n + 3) // RING + 1, items_of(n + 1), HEAD)
            values(STEPS - 1, RING - 1, TT - 1)
            direct_sum(STEPS - 1, TT - 1)
            last_sum(STEPS - 1)

            pe.wait_ge(bt_done, STEPS)
            pe.wait_ge(mx_freed, PRO_VECTOR_ITEMS + STEP_VECTOR_ITEMS * (STEPS - 2) + EARLY)
            with pe.Fori(0, GROUPS // 2) as i:
                for par in range(2):
                    o = 2 * i + par
                    pe.wait_ge(wo_in[par], 16 * (i + 1))
                    pe.wait_ge(wo_lo, o + 1)
                    for k in range(KCH):
                        ins = nc.tensor.transpose(MX[par][:, k * P:(k + 1) * P], WS[par][:, k * P:(k + 1) * P], ident[:, :])
                    ins.then_inc(wo_ready, 1)
            pe.wait_ge(wo_lo, 2 + GROUPS)

            def project_out(t, q):
                pe.wait_ge(al_done, t + 1)
                for half in range(2):
                    cs = slice(half * 512, (half + 1) * 512)
                    ops = [(AH, WOh), (AL, WOh), (AH, WOl)]
                    for g in range(GROUPS):
                        for o, (a, w) in enumerate(ops):
                            ins = nc.tensor.matmul(MX[q][:, cs], a[q][:, g, :], w[:, g, cs],
                                                   start=(g == 0 and o == 0), stop=(g == GROUPS - 1 and o == 2))
                    ins.then_inc(o_ready, 1)

            with pe.Fori(0, TOK_TILES // 2) as i:
                for q in range(2):
                    project_out(2 * i + q, q)


_INS = ["x", "ctx_4096", "mask_BxS2_bf1", "L0_xattn_Wq", "L0_xattn_Wout", "L0_xattn_ln_gamma", "L0_xattn_ln_beta"]


def kernel(**inputs):
    import numpy as _np
    import concourse.bacc as _bacc
    from concourse import mybir as _mybir
    from concourse.bass_utils import run_bass_kernel_spmd as _run

    nc = _bacc.Bacc("TRN2", target_bir_lowering=False, num_devices=1)
    arrays, args = {}, []
    for name in _INS:
        a = _np.ascontiguousarray(inputs[name])
        if a.dtype == _np.bool_:
            a = a.view(_np.uint8)
        arrays[f"in_{name}"] = a
        args.append(nc.dram_tensor(f"in_{name}", a.shape, _mybir.dt.from_np(a.dtype), kind="ExternalInput").ap())
    out = nc.dram_tensor("out_0", (BATCH, S, HID), F32, kind="ExternalOutput").ap()
    build(nc, *args, out)
    r = _run(nc, [arrays], core_ids=[0])
    return r.results[0]["out_0"]
```

```python
import numpy as np
import concourse.bass as bass
from concourse import mybir

F32 = mybir.dt.float32
F32R = mybir.dt.float32r
BF16 = mybir.dt.bfloat16
U8 = mybir.dt.uint8
ALU = mybir.AluOpType
ACT = mybir.ActivationFunctionType

BATCH, S, HID = 2, 512, 1024
T = 1024
HD = 32
P = 128
HPG = P // HD
GROUPS = HID // P
STEPS = GROUPS * BATCH
TOK = BATCH * S
TOK_TILES = TOK // P
KCH = HID // P
TT = T // P
ST = S // P
RING = 4
BIAS = 3 * HD
ROWS = BIAS + 2
SCALE = float(HD) ** -0.5
EPS = 1e-5
BIG = 3.0e38
POOL_TILES = (0, 1, 2, 4, 5, 6)
ADDS = len(POOL_TILES) - 1
SUM_SLOT = 1

DVE_T = 32

M_ITEMS = HPG * ST
EARLY = ST



def keys(a):
    return [("keys", a, 0)]


def maxima(a, *items):
    return [("max", a, i) for i in items]


def bias(a):
    return [("bias", a, 0)]


FIRST_STEP = [
    ([], []),
    ([], maxima(1, 0, 1)),
    (maxima(1, 2), maxima(1, 3, 4)),
    (maxima(1, 5), keys(2) + maxima(1, 6)),
    (maxima(1, 7), maxima(1, 8, 9)),
    (maxima(1, 10), maxima(1, 11, 12)),
    (maxima(1, 13), maxima(1, 14, 15)),
    (maxima(2, 0), bias(1) + maxima(2, 1, 2, 3)),
]
STEP = [
    ([], keys(2)),
    (maxima(1, 4), maxima(1, 5, 6)),
    ([], maxima(1, 7, 8)),
    ([], maxima(1, 9, 10)),
    (maxima(1, 11), maxima(1, 12, 13)),
    ([], maxima(1, 14, 15)),
    ([], maxima(2, 0) + bias(1)),
    (maxima(2, 1), maxima(2, 2, 3)),
]
SUMS_AT = (2, 4, 7)


def is_first(n):
    return isinstance(n, int) and n == 0


def items_of(n):
    return [tuple([i for i in part if n + i[1] < STEPS] for part in slot) for slot in (FIRST_STEP if n == 0 else STEP)]


def flat(items):
    return [i for slot in items for part in slot for i in part]


def vector_items(items):
    return sum(i[0] != "bias" for i in flat(items))


WITH_GROUP = [[("wq", 1)]]
for _g, (_i, _k) in enumerate([(0, 2), (2, 4), (6, 3), (9, 3), (12, 3), (15, 1)]):
    WITH_GROUP.append([("wq", _g + 2)] + [("max", _i + k) for k in range(_k)])
WITH_GROUP.append([("bias", 0), ("keys", 1)])
ORDER = [("wq", 0), ("keys", 0)] + [i for items in WITH_GROUP for i in items]
BUFFER = {item: at % 2 for at, item in enumerate(ORDER)}
FIRST_PARITY = len(ORDER) % 2
BEFORE = 2 + M_ITEMS
BEFORE_1 = BEFORE + vector_items(FIRST_STEP)
PER_STEP = vector_items(STEP)
STEP_PARITY = (FIRST_PARITY + len(flat(FIRST_STEP))) % 2


def vector_freed(n):
    return BEFORE_1 + PER_STEP * (n - 1)


def build(nc, x, ctx, mask, wq, wout, gamma, beta, out):
    def sb(name, shape, dt):
        return nc.alloc_sbuf_tensor(name, shape, dt)

    ident = sb("ident", [P, P], F32)
    ones = sb("ones", [P, HD], F32)
    QA = sb("QA", [P, STEPS, S], F32)
    R = sb("R", [P, RING * HPG * (T + S)], F32R)
    KSZ, QSZ = HPG * T, HPG * S
    q_at = {2: RING * KSZ, 3: RING * KSZ + QSZ, 1: RING * KSZ + 2 * QSZ, 0: RING * KSZ + 3 * QSZ}
    KS = [R[:, r * KSZ:(r + 1) * KSZ].rearrange("p (h t) -> p h t", h=HPG) for r in range(RING)]
    QS = [R[:, q_at[r]:q_at[r] + QSZ].rearrange("p (h s) -> p h s", h=HPG) for r in range(RING)]
    XTh = [R[:, at:at + KCH * S].rearrange("p (k s) -> p k s", k=KCH) for at in (KSZ, 3 * KSZ)]
    XTl = [R[:, at:at + KCH * S].rearrange("p (k s) -> p k s", k=KCH) for at in (2 * KSZ, q_at[2])]
    KTh = sb("KTh", [P, T], F32R)
    KTl = sb("KTl", [P, T], F32R)
    WTh = [KTh[:, :], R[:, q_at[1]:q_at[1] + HID]]
    WTl = [KTl[:, :], R[:, q_at[1] + HID:q_at[1] + 2 * HID]]
    WOh = R[:, 0:KCH * HID].rearrange("p (k s) -> p k s", k=KCH)
    WOl = R[:, KCH * HID:2 * KCH * HID].rearrange("p (k s) -> p k s", k=KCH)
    a0 = 2 * KCH * HID
    AH = [R[:, a0 + q * HID:a0 + (q + 1) * HID].rearrange("p (g n) -> p g n", g=GROUPS) for q in range(2)]
    AL = [R[:, a0 + (2 + q) * HID:a0 + (3 + q) * HID].rearrange("p (g n) -> p g n", g=GROUPS) for q in range(2)]
    C = [sb(f"C{r}", [P, TT, P], F32) for r in range(RING)]
    YT = [C[3][:, 4 * i:4 * i + 4, :].rearrange("p a c -> p (a c)") for i in range(2)]
    PR = sb("PR", [P, RING, HPG, S], F32)
    XS = PR[:, :, :, :].rearrange("p a b c -> p (a b c)").rearrange("p (t c) -> p t c", t=TOK_TILES)
    acc = sb("acc", [P, HPG, S], F32)
    WS = [acc[:, 2 * g:2 * g + 2, :].rearrange("p a b -> p (a b)") for g in range(2)]
    QTh = sb("QTh", [P, S], F32R)
    QTl = sb("QTl", [P, S], F32R)
    rsum = sb("rsum", [P, S], F32)
    warm = sb("warm", [P, 1], F32)
    rcol = sb("rcol", [P, S // DVE_T], F32)
    BT = sb("BT", [2 * HPG, S], F32R)
    maskadd = sb("maskadd", [P, BATCH, T], BF16)
    maskrow = rsum[:, :].bitcast(U8).rearrange("p (b t) -> p b t", b=BATCH)
    mx = sb("mx", [P, 2, M_ITEMS], F32)
    mxh = sb("mxh", [P, 2, M_ITEMS], F32R)
    MM = sb("MM", [P, (ST - 1) * 2 * HPG + P], F32)
    onesrow = QA[0:2, STEPS // 2:STEPS // 2 + 8, :]
    aux = sb("aux", [P, P], F32)
    auxm = sb("auxm", [P, P], U8)
    cols = sb("cols", [P, P], F32)
    stats = sb("stats", [P, TOK_TILES, 2, 6], F32)
    mv = sb("mv", [P, TOK_TILES, 2], F32)
    veps = sb("veps", [P, TOK_TILES], F32)
    sd = sb("sd", [P, TOK_TILES], F32)
    rstd = sb("rstd", [P, TOK_TILES], F32)
    newt = sb("newt", [P, TOK_TILES], F32)
    nmr = sb("nmr", [P, TOK_TILES], F32)
    GAM, BET, MSK = 0, 32, 64

    MX = [nc.alloc_psum_tensor(f"MX{i}", [P, T], F32) for i in range(2)]
    SX = [nc.alloc_psum_tensor(f"SX{i}", [P, S], F32) for i in range(2)]
    PV = nc.alloc_psum_tensor("PV", [P, S], F32)
    SM = nc.alloc_psum_tensor("SM", [P, S], F32)
    QP = [PV, SM]

    sem = nc.alloc_semaphore
    const_done = sem("const_done")
    aux_in, aux_ready, aux_t, cols_ready = sem("aux_in"), sem("aux_ready"), sem("aux_t"), sem("cols_ready")
    maskrow_in, mask_ready = sem("maskrow_in"), sem("mask_ready")
    onesrow_ready, onesrow_in = sem("onesrow_ready"), sem("onesrow_in")
    x_in = [sem(f"x_in{t}") for t in range(TOK_TILES)]
    chain = sem("chain")
    var_ready, sd_ready, norm_ready, xn_ready = sem("var_ready"), sem("sd_ready"), sem("norm_ready"), sem("xn_ready")
    xt_ready, y_ready, xt_split = sem("xt_ready"), sem("y_ready"), sem("xt_split")
    w_in = [sem(f"w_in{g}") for g in range(2)]
    wt_ready, wt_hi, wt_lo, q_done, q_copied = sem("wt_ready"), sem("wt_hi"), sem("wt_lo"), sem("q_done"), sem("q_copied")
    c_in = [sem(f"c_in{r}") for r in range(RING)]
    kt_ready, kt_hi, kt_lo, qt_hi, qt_lo = sem("kt_ready"), sem("kt_hi"), sem("kt_lo"), sem("qt_hi"), sem("qt_lo")
    stack_in = [sem(f"stack_in{h}") for h in range(HPG)]
    m_ready, mx_freed, mm_ready, bt_ready, bt_done = (
        sem("m_ready"), sem("mx_freed"), sem("mm_ready"), sem("bt_ready"), sem("bt_done"))
    bias_in = [sem(f"bias_in{h}") for h in range(HPG)]
    sums_turned, recip_ready = sem("sums_turned"), sem("recip_ready")
    scores_ready, exp_done, tile_used, pool_used = sem("scores_ready"), sem("exp_done"), sem("tile_used"), sem("pool_used")
    gate = sem("gate")
    pv_done, pv_copied, sums_done, rsum_done, attn_done = (
        sem("pv_done"), sem("pv_copied"), sem("sums_done"), sem("rsum_done"), sem("attn_done"))
    wo_in = [sem(f"wo_in{g}") for g in range(2)]
    wo_ready, wo_hi, wo_lo = sem("wo_ready"), sem("wo_hi"), sem("wo_lo")
    xr_in = [sem(f"xr_in{q}") for q in range(2)]
    ah_done, al_done, o_ready, o_added = sem("ah_done"), sem("al_done"), sem("o_ready"), sem("o_added")
    out_in = [sem(f"out_in{q}") for q in range(2)]

    ctx_v = ctx.rearrange("b (t p) (g c) -> p b t g c", p=P, c=P)
    xt_v = x.rearrange("b (t p) c -> p (b t) c", p=P)
    out_v = out.rearrange("b (t p) c -> p (b t) c", p=P)
    wq_v = wq.rearrange("(g p) c -> p g c", p=P)
    wo_v = wout.rearrange("(g p) c -> p g c", p=P)
    QAt = QA[:, :, :].rearrange("p (g b) s -> p g (b s)", b=BATCH)

    LOOPS = STEPS // RING - 1
    APART = range(LOOPS * RING + 1, STEPS)

    with nc.Block() as block:

        @block.sync
        def _(sp):
            def load_values(r, b, g):
                sp.dma_start(C[r][:, :, :], ctx_v[:, b, :, bass.ds(g, 1), :].rearrange("p t a c -> p t (a c)")).then_inc(c_in[r], 16)

            def load_wq(par, g):
                sp.dma_start(WS[par], wq_v[:, bass.ds(g, 1), :].rearrange("p a c -> p (a c)")).then_inc(w_in[par], 16)

            for t in range(ST):
                sp.dma_start(XS[:, t, :], xt_v[:, t, :]).then_inc(x_in[t], 16)
            load_values(0, 0, 0)
            load_wq(0, 0)
            for t in range(ST, TOK_TILES):
                sp.dma_start(XS[:, t, :], xt_v[:, t, :]).then_inc(x_in[t], 16)
            load_wq(1, 1)
            load_values(1, 1, 0)
            load_values(2, 0, 1)

            def key_rows(r, h):
                own = slice(h * HD, (h + 1) * HD)
                sp.dma_start(KS[r][0:HD, h, :].bitcast(F32), KTh[own, :].bitcast(F32)).then_inc(stack_in[h], 16)
                sp.dma_start(KS[r][HD:2 * HD, h, :].bitcast(F32), KTl[own, :].bitcast(F32)).then_inc(stack_in[h], 16)
                sp.dma_start(KS[r][2 * HD:3 * HD, h, :].bitcast(F32), KTh[own, :].bitcast(F32)).then_inc(stack_in[h], 16)

            def query_rows(r, h):
                own = slice(h * HD, (h + 1) * HD)
                sp.dma_start(QS[r][0:HD, h, :].bitcast(F32), QTh[own, :].bitcast(F32)).then_inc(stack_in[h], 16)
                sp.dma_start(QS[r][HD:2 * HD, h, :].bitcast(F32), QTh[own, :].bitcast(F32)).then_inc(stack_in[h], 16)
                sp.dma_start(QS[r][2 * HD:3 * HD, h, :].bitcast(F32), QTl[own, :].bitcast(F32)).then_inc(stack_in[h], 16)

            def keys_split(n):
                sp.wait_ge(kt_hi, n + 1)
                sp.wait_ge(kt_lo, n + 1)

            def queries_split(n):
                sp.wait_ge(qt_hi, n + 1)
                sp.wait_ge(qt_lo, n + 1)

            def stack(n, u):
                queries_split(n)
                keys_split(n)
                for h in range(HPG):
                    key_rows(u % RING, h)
                    query_rows(u % RING, h)

            def bias_rows(n, u):
                r = u % RING
                sp.wait_ge(bt_done, n + 1)
                for h in range(HPG):
                    sp.dma_start(QS[r][BIAS:ROWS, h, :].bitcast(F32), BT[2 * h:2 * h + 2, :].bitcast(F32)).then_inc(bias_in[h], 16)

            def next_wq(par, g):
                sp.wait_ge(wt_ready, g + 1)
                load_wq(par, g + 2)

            keys_split(0)
            for h in range(HPG):
                key_rows(0, h)
            sp.wait_ge(onesrow_ready, 1)
            sp.dma_start(KS[0][BIAS:ROWS, :, :].rearrange("p h t -> p (h t)").bitcast(F32),
                         onesrow.rearrange("p n s -> p (n s)")).then_inc(onesrow_in, 16)
            next_wq(0, 0)
            next_wq(1, 1)
            queries_split(0)
            for h in range(HPG):
                query_rows(0, h)
            with sp.Fori(1, GROUPS // 2 - 1) as i:
                for g in range(2):
                    next_wq(g, 2 * i + g)
            bias_rows(0, 0)
            sp.wait_ge(q_done, BATCH * GROUPS - 1)
            keys_split(1)
            for h in range(2):
                key_rows(1, h)
            queries_split(1)
            sp.wait_ge(q_done, BATCH * GROUPS)
            for h in range(2):
                query_rows(1, h)
            for h in range(2, HPG):
                key_rows(1, h)
                query_rows(1, h)
            sp.wait_ge(onesrow_in, 16)
            for r in range(1, RING):
                sp.dma_start(KS[r][BIAS:ROWS, :, :].bitcast(F32), KS[0][BIAS:ROWS, :, :].bitcast(F32)).then_inc(onesrow_in, 16)
            load_values(3, 1, 1)
            stack(2, 2)
            bias_rows(1, 1)

            def step(n, u, g, values, stacks, bias):
                if values:
                    sp.wait_ge(pv_done, n)
                    load_values((u + 3) % RING, (u + 3) % BATCH, g)
                if stacks:
                    stack(n + 2, u + 2)
                if bias:
                    bias_rows(n + 1, u + 1)

            with sp.Fori(0, LOOPS) as j:
                for u in range(1, RING + 1):
                    step(RING * j + u, u, 2 * j + (u + 3) // BATCH, True, True, True)
            for n in APART:
                step(n, n % RING, (n + 3) // BATCH, n + 3 < STEPS, n + 2 < STEPS, n + 1 < STEPS)
            sp.wait_ge(sums_done, STEPS)
            for g in range(2):
                sp.dma_start(WS[g], wo_v[:, g, :]).then_inc(wo_in[g], 16)
            for q in range(2):
                sp.dma_start(XS[:, q, :], xt_v[:, q, :]).then_inc(xr_in[q], 16)
            with sp.Fori(0, GROUPS // 2 - 1) as i:
                for g in range(2):
                    sp.wait_ge(wo_ready, 2 * i + g + 1)
                    sp.dma_start(WS[g], wo_v[:, bass.ds(2 * i + g + 2, 1), :].rearrange("p a c -> p (a c)")).then_inc(wo_in[g], 16)

            def store(t, q):
                sp.wait_ge(o_added, 2 * t + 2)
                sp.dma_start(out_v[:, bass.ds(t, 1), :].rearrange("p a c -> p (a c)"), XS[:, 2 + q, :]).then_inc(out_in[q], 16)

            with sp.Fori(0, TOK_TILES // 2 - 1) as i:
                for q in range(2):
                    t = 2 * i + q
                    store(t, q)
                    sp.dma_start(XS[:, q, :], xt_v[:, bass.ds(t + 2, 1), :].rearrange("p a c -> p (a c)")).then_inc(xr_in[q], 16)
            for q in range(2):
                store(TOK_TILES - 2 + q, q)
            for q in range(2):
                sp.wait_ge(out_in[q], 16 * TOK_TILES // 2)

        @block.gpsimd
        def _(pool):
            pool.sem_inc(attn_done, 1)
            nc.gpsimd.memset(aux[:, :], 0.0).then_inc(const_done, 1)
            nc.gpsimd.memset(ident[:, :], 0.0).then_inc(const_done, 1)
            nc.gpsimd.memset(ones[:, :], 1.0).then_inc(const_done, 1)
            pool.wait_ge(const_done, 3)
            nc.gpsimd.affine_select(out=ident[:, :], in_=ident[:, :], compare_op=ALU.not_equal, fill=1.0,
                                    base=0, pattern=[[-1, P]], channel_multiplier=1).then_inc(const_done, 1)
            pool.dma_start(maskrow, mask.rearrange("b t -> (b t)").partition_broadcast(P).rearrange("p (b t) -> p b t", b=BATCH)).then_inc(maskrow_in, 16)
            nc.gpsimd.memset(MM[:, :], 0.0).then_inc(const_done, 1)
            nc.gpsimd.memset(onesrow, 1.0).then_inc(onesrow_ready, 1)

            pool.sem_inc(pool_used, ADDS)

            def normalise(n):
                pool.wait_ge(pv_copied, n + 1)
                pool.wait_ge(rsum_done, n + 1)
                pool.sem_inc(gate, 1)
                at = QA[:, bass.ds(n, 1), :].rearrange("p a s -> p (a s)")
                nc.gpsimd.tensor_tensor(at, at, rsum[:, :], ALU.mult).then_inc(attn_done, 1)

            def add_probs(n, k):
                first, tt = POOL_TILES[0], POOL_TILES[k + 1]
                if is_first(n) and k == 0:
                    pass
                elif k == 0:
                    pool.wait_ge(sums_done, n)
                else:
                    pool.wait_ge(pool_used, ADDS * n + ADDS + k)
                pool.wait_ge(exp_done, 2 + TT * HPG * n + HPG * (tt + 1))
                a = PR[:, first % RING, :, :] if k == 0 else acc[:, :, :]
                nc.gpsimd.tensor_tensor(acc[:, :, :], a, PR[:, tt % RING, :, :], ALU.add).then_inc(pool_used, 1)

            def step(n):
                for k in range(ADDS):
                    add_probs(n, k)
                if not is_first(n):
                    normalise(n - 1)

            step(0)
            with pool.Fori(0, LOOPS) as j:
                for u in range(1, RING + 1):
                    step(RING * j + u)
            for n in APART:
                step(n)
            normalise(STEPS - 1)

        @block.scalar
        def _(act):
            act.wait_ge(const_done, 1)
            act.dma_start(aux[GAM:GAM + KCH, :], gamma.rearrange("(k p) -> k p", p=P)).then_inc(aux_in, 16)
            act.dma_start(aux[BET:BET + KCH, :], beta.rearrange("(k p) -> k p", p=P)).then_inc(aux_in, 16)
            act.dma_start(auxm[MSK:MSK + BATCH * TT, :], mask.rearrange("b (t p) -> (b t) p", p=P)).then_inc(aux_in, 16)

            def deviations(b):
                act.wait_ge(var_ready, b + 1)
                ts = slice(b * ST, (b + 1) * ST)
                nc.scalar.activation(sd[:, ts], veps[:, ts], ACT.Sqrt).then_inc(sd_ready, 1)

            def normalised(b):
                act.wait_ge(norm_ready, b + 1)
                for t in range(b * ST, (b + 1) * ST):
                    nc.scalar.activation(XS[:, t, :], XS[:, t, :], ACT.Identity, scale=rstd[:, t:t + 1],
                                         bias=nmr[:, t:t + 1]).then_inc(xn_ready, 1)

            def scaled(i):
                k = i % KCH
                act.wait_ge(xt_ready, i + 1)
                if i >= 2:
                    act.wait_ge(xt_split, i - 1)
                nc.scalar.activation(YT[i % 2], SX[i % 2][:, :], ACT.Identity, scale=cols[:, GAM + k:GAM + k + 1],
                                     bias=cols[:, BET + k:BET + k + 1]).then_inc(y_ready, 1)

            def key_high(n, par):
                act.wait_ge(kt_ready, n + 1)
                if not is_first(n):
                    for h in range(HPG):
                        act.wait_ge(stack_in[h], 96 * n)
                nc.scalar.activation(KTh[:, :], MX[par][:, :], ACT.Copy).then_inc(kt_hi, 1)

            deviations(0)
            normalised(0)
            key_high(0, BUFFER["keys", 0])
            act.wait_ge(cols_ready, 1)
            for i in range(KCH // 2):
                scaled(i)
            deviations(1)
            for i in range(KCH // 2, KCH):
                scaled(i)
            normalised(1)
            for i in range(KCH, 2 * KCH):
                scaled(i)

            def wt_high(g):
                act.wait_ge(wt_ready, g + 1)
                nc.scalar.activation(WTh[g % 2], MX[BUFFER["wq", g]][:, :], ACT.Copy).then_inc(wt_hi, 1)

            def q_copy(g):
                for b in range(BATCH):
                    act.wait_ge(q_done, BATCH * g + b + 1)
                    nc.scalar.activation(QA[:, bass.ds(BATCH * g + b, 1), :].rearrange("p a s -> p (a s)"),
                                         QP[b][:, :], ACT.Copy).then_inc(q_copied, 1)

            act.sem_inc(q_copied, 2)
            act.wait_ge(onesrow_in, 16)
            def bias_copy(n, par):
                act.wait_ge(bt_ready, n + 1)
                if not is_first(n):
                    for h in range(HPG):
                        act.wait_ge(bias_in[h], 16 * n)
                nc.scalar.activation(BT[:, :], MX[par][0:2 * HPG, 0:S], ACT.Copy).then_inc(bt_done, 1)

            for h in range(HPG):
                act.wait_ge(stack_in[h], 3 * 16)
            wt_high(0)
            for g in range(GROUPS):
                if g + 1 < GROUPS:
                    if g >= 1:
                        act.wait_ge(q_done, BATCH * g)
                    wt_high(g + 1)
                else:
                    bias_copy(0, BUFFER["bias", 0])
                    act.wait_ge(q_done, BATCH * g)
                    nc.scalar.activation(warm[:, :], cols[:, 0:1], ACT.Exp)
                    key_high(1, BUFFER["keys", 1])
                q_copy(g)

            def exps(n, u, tt, pair):
                for h in (2 * pair, 2 * pair + 1):
                    q = TT * HPG * n + HPG * tt + h
                    if h == 0:
                        act.wait_ge(tile_used, TT * n + tt + 1)
                        old, m = (tt - RING, n) if tt >= RING else (tt + RING, n - 1)
                        if old in POOL_TILES:
                            act.wait_ge(pool_used, ADDS * m + ADDS + max(POOL_TILES.index(old), 1))
                    act.wait_ge(scores_ready, q + 1)
                    b = u % BATCH
                    nc.scalar.activation(PR[:, tt % RING, h, :], SX[h % 2][:, :], ACT.Exp, scale=SCALE,
                                         bias=cols[:, MSK + b * TT + tt:MSK + b * TT + tt + 1]).then_inc(exp_done, 1)

            act.sem_inc(exp_done, 2)

            def pv_copy(n):
                act.wait_ge(pv_done, n + 1)
                nc.scalar.activation(QA[:, bass.ds(n, 1), :].rearrange("p a s -> p (a s)"), PV[:, :], ACT.Copy).then_inc(pv_copied, 1)

            def high_and_bias(n, items, at):
                for kind, a, i in items:
                    if kind == "keys":
                        key_high(n + a, at % 2)
                    if kind == "bias":
                        bias_copy(n + a, at % 2)
                    at += 1
                return at

            def step(n, u, items, at, first=False):
                for tt in range(TT):
                    exps(n, u, tt, 0)
                    if tt == 0 and not first:
                        pv_copy(n - 1)
                    at = high_and_bias(n, items[tt][0], at)
                    exps(n, u, tt, 1)
                    at = high_and_bias(n, items[tt][1], at)

            step(0, 0, FIRST_STEP, FIRST_PARITY, first=True)
            with act.Fori(0, LOOPS) as j:
                for u in range(1, RING + 1):
                    step(RING * j + u, u, STEP, STEP_PARITY)
            for n in APART:
                step(n, n % RING, items_of(n), STEP_PARITY)
            pv_copy(STEPS - 1)

            with act.Fori(0, GROUPS // 2) as i:
                for par in range(2):
                    o = 2 * i + par
                    act.wait_ge(wo_ready, o + 1)
                    nc.scalar.activation(WOh[:, :, bass.ds(o * P, P)], MX[par][:, :].rearrange("p (g n) -> p g n", n=P),
                                         ACT.Copy).then_inc(wo_hi, 1)

        @block.vector
        def _(dve):
            links = [0]

            def link(ins):
                links[0] += 1
                ins.then_inc(chain, 1)
                dve.wait_ge(chain, links[0])


            def statistics(b):
                ts = slice(b * ST, (b + 1) * ST)
                for t in range(b * ST, (b + 1) * ST):
                    dve.wait_ge(x_in[t], 16)
                    for half in range(2):
                        ins = nc.vector.bn_stats(stats[:, t, half, :], XS[:, t, half * 512:(half + 1) * 512])
                link(ins)
                for t in range(b * ST, (b + 1) * ST):
                    ins = nc.vector.bn_aggr(mv[:, t, :], stats[:, t, :, :].rearrange("p a b -> p (a b)"))
                link(ins)
                nc.vector.tensor_scalar(veps[:, ts], mv[:, ts, 1], EPS, None, ALU.add).then_inc(var_ready, 1)

            def norm_factors(b):
                ts = slice(b * ST, (b + 1) * ST)
                dve.wait_ge(sd_ready, b + 1)
                link(nc.vector.reciprocal(rstd[:, ts], sd[:, ts]))
                link(nc.vector.tensor_tensor(newt[:, ts], rstd[:, ts], rstd[:, ts], ALU.mult))
                link(nc.vector.tensor_tensor(newt[:, ts], newt[:, ts], veps[:, ts], ALU.mult))
                link(nc.vector.tensor_scalar(newt[:, ts], newt[:, ts], -0.5, 1.5, ALU.mult, ALU.add))
                link(nc.vector.tensor_tensor(rstd[:, ts], rstd[:, ts], newt[:, ts], ALU.mult))
                nc.vector.scalar_tensor_tensor(nmr[:, ts], mv[:, ts, 0], -1.0, rstd[:, ts], ALU.mult, ALU.mult).then_inc(norm_ready, 1)

            def split_x(i):
                b, k = divmod(i, KCH)
                dve.wait_ge(y_ready, i + 1)
                link(nc.vector.tensor_copy(XTh[b][:, k, :], YT[i % 2]))
                nc.vector.tensor_tensor(XTl[b][:, k, :], YT[i % 2], XTh[b][:, k, :].bitcast(F32), ALU.subtract).then_inc(xt_split, 1)

            def key_low(n, par):
                dve.wait_ge(kt_hi, n + 1)
                nc.vector.tensor_tensor(KTl[:, :], MX[par][:, :], KTh[:, :].bitcast(F32), ALU.subtract).then_inc(kt_lo, 1)
                dve.wait_ge(kt_lo, n + 1)
                dve.sem_inc(mx_freed, 1)

            statistics(0)
            norm_factors(0)
            dve.wait_ge(aux_in, 48)
            dve.wait_ge(const_done, 5)
            nc.vector.tensor_scalar(aux[MSK:MSK + BATCH * TT, :], auxm[MSK:MSK + BATCH * TT, :], BIG, -BIG,
                                    ALU.mult, ALU.add).then_inc(aux_ready, 1)
            dve.wait_ge(aux_t, 1)
            nc.vector.tensor_copy(cols[:, :], SM[:, 0:P]).then_inc(cols_ready, 1)
            key_low(0, BUFFER["keys", 0])
            statistics(1)
            for i in range(KCH // 2):
                split_x(i)
            norm_factors(1)
            for i in range(KCH // 2, 2 * KCH):
                split_x(i)
            dve.wait_ge(maskrow_in, 16)
            for b in range(BATCH):
                ins = nc.vector.tensor_scalar(maskadd[:, b, :], maskrow[:, b, :], BIG, -BIG, ALU.mult, ALU.add)
            link(ins)

            def w_low(g):
                dve.wait_ge(wt_hi, g + 1)
                nc.vector.tensor_tensor(WTl[g % 2], MX[BUFFER["wq", g]][:, :], WTh[g % 2].bitcast(F32), ALU.subtract).then_inc(wt_lo, 1)

            def split_queries(n):
                if not is_first(n):
                    for h in range(HPG):
                        dve.wait_ge(stack_in[h], 96 * n)
                q = QA[:, bass.ds(n, 1), :].rearrange("p a s -> p (a s)")
                nc.vector.tensor_copy(QTh[:, :], q).then_inc(qt_hi, 1)
                dve.wait_ge(qt_hi, n + 1)
                nc.vector.tensor_tensor(QTl[:, :], q, QTh[:, :].bitcast(F32), ALU.subtract).then_inc(qt_lo, 1)

            def maximum(n, u, i, par):
                h, st = divmod(i, ST)
                c = st * HPG + h
                dve.wait_ge(m_ready, M_ITEMS * n + i + 1)
                dve.sem_inc(gate, 1)
                nc.vector.tensor_tensor_reduce(out=MX[par][:, :], in0=MX[par][:, :], in1=maskadd[:, u % BATCH, :], scale=1.0,
                                               scalar=-BIG, op0=ALU.add, op1=ALU.max,
                                               accum_out=mx[:, u % 2, c:c + 1]).then_inc(mx_freed, 1)

            def bias_columns(n, u, freed):
                dve.wait_ge(mx_freed, freed)
                if not is_first(n):
                    dve.wait_ge(bt_ready, n)
                nc.vector.tensor_scalar(mxh[:, u % 2, :], mx[:, u % 2, :], -1.0, None, ALU.mult).then_inc(mm_ready, 1)
                dve.wait_ge(mm_ready, 3 * n + 1)
                hi = mxh[:, u % 2, :].bitcast(F32)
                cols_of = MM[:, 0:ST * 2 * HPG].rearrange("p (s h a) -> p s h a", h=HPG, a=2)
                nc.vector.tensor_copy(cols_of[:, :, :, 0], hi.rearrange("p (s h) -> p s h", h=HPG)).then_inc(mm_ready, 1)
                nc.vector.scalar_tensor_tensor(cols_of[:, :, :, 1], mx[:, u % 2, :].rearrange("p (s h) -> p s h", h=HPG), -1.0,
                                               hi.rearrange("p (s h) -> p s h", h=HPG), ALU.mult, ALU.subtract).then_inc(mm_ready, 1)

            def invert_sums(n, part):
                if part == 0:
                    dve.wait_ge(sums_done, n + 1)
                    dve.wait_ge(attn_done, 1 + n)
                    nc.vector.transpose(rsum[:, :], SM[:, :]).then_inc(sums_turned, 1)
                if part == 1:
                    dve.wait_ge(sums_turned, n + 1)
                    nc.vector.reciprocal(rcol[:, :], rsum[:, :].rearrange("p (b i) -> p b i", i=DVE_T)[:, :, 0]).then_inc(recip_ready, 1)
                if part == 2:
                    dve.wait_ge(recip_ready, n + 1)
                    nc.vector.transpose(rsum[:, :].rearrange("p (b i) -> p b i", i=DVE_T),
                                        rcol[:, :].unsqueeze(2).to_broadcast([P, S // DVE_T, DVE_T])).then_inc(rsum_done, 1)

            w_low(0)
            for g in range(GROUPS):
                if g == 1:
                    dve.wait_ge(q_copied, 2 + 1)
                    split_queries(0)
                for item in WITH_GROUP[g]:
                    if item[0] == "wq":
                        w_low(item[1])
                    if item[0] == "max":
                        maximum(0, 0, item[1], BUFFER[item])
                if g == GROUPS - 4:
                    split_queries(1)
            bias_columns(0, 0, BEFORE - 1)
            key_low(1, BUFFER["keys", 1])

            def step(n, u, items, at, freed, first=False):
                for tt in range(TT):
                    parts = [SUMS_AT.index(tt)] if tt in SUMS_AT and not first else []
                    for kind, a, i in items[tt][0] + items[tt][1]:
                        if kind == "keys":
                            if a == 2:
                                split_queries(n + a)
                            key_low(n + a, at % 2)
                            freed = freed + 1
                        if kind == "max":
                            maximum(n + a, u + a, i, at % 2)
                            freed = freed + 1
                            if i == M_ITEMS - 1:
                                bias_columns(n + a, u + a, freed)
                        at += 1
                        if parts:
                            invert_sums(n - 1, parts.pop())
                    if parts:
                        invert_sums(n - 1, parts.pop())

            step(0, 0, FIRST_STEP, FIRST_PARITY, BEFORE, first=True)
            with dve.Fori(0, LOOPS) as j:
                for u in range(1, RING + 1):
                    n = RING * j + u
                    step(n, u, STEP, STEP_PARITY, vector_freed(n))
            for n in APART:
                step(n, n % RING, items_of(n), STEP_PARITY, vector_freed(n))
            for part in range(3):
                invert_sums(STEPS - 1, part)
            dve.sem_inc(wo_lo, 2)

            with dve.Fori(0, GROUPS // 2) as i:
                for par in range(2):
                    o = 2 * i + par
                    dve.wait_ge(wo_hi, o + 1)
                    nc.vector.tensor_tensor(WOl[:, :, bass.ds(o * P, P)], MX[par][:, :].rearrange("p (g n) -> p g n", n=P),
                                            WOh[:, :, bass.ds(o * P, P)].bitcast(F32), ALU.subtract).then_inc(wo_lo, 1)
            dve.wait_ge(attn_done, 1 + STEPS)

            def split_attn(t, q):
                src = QAt[:, :, bass.ds(t * P, P)]
                nc.vector.tensor_copy(AH[q][:, :, :], src).then_inc(ah_done, 1)
                dve.wait_ge(ah_done, t + 1)
                nc.vector.tensor_tensor(AL[q][:, :, :], src, AH[q][:, :, :].bitcast(F32), ALU.subtract).then_inc(al_done, 1)

            def add_residual(t, i, q, stored=True):
                dve.wait_ge(xr_in[q], 16 * (i + 1))
                if stored:
                    dve.wait_ge(out_in[q], 16 * i)
                for half in range(2):
                    dve.wait_ge(o_ready, 2 * t + half + 1)
                    cs = slice(half * 512, (half + 1) * 512)
                    nc.vector.tensor_tensor(XS[:, 2 + q, cs], XS[:, q, cs], MX[q][:, cs], ALU.add).then_inc(o_added, 1)

            split_attn(0, 0)
            split_attn(1, 1)
            for q in range(2):
                add_residual(q, 0, q, stored=False)
                split_attn(q + 2, q)
            with dve.Fori(1, TOK_TILES // 2 - 1) as i:
                for q in range(2):
                    add_residual(2 * i + q, i, q)
                    split_attn(2 * i + q + 2, q)
            for q in range(2):
                add_residual(TOK_TILES - 2 + q, TOK_TILES // 2 - 1, q)

        @block.tensor
        def _(pe):
            pe.wait_ge(const_done, 5)

            def wt_transposes(g):
                pe.wait_ge(w_in[g % 2], 16 * (g // 2 + 1))
                for k in range(KCH):
                    ins = nc.tensor.transpose(MX[BUFFER["wq", g]][:, k * P:(k + 1) * P], WS[g % 2][:, k * P:(k + 1) * P], ident[:, :])
                ins.then_inc(wt_ready, 1)

            def keys_item(n, u, par, loads):
                pe.wait_ge(c_in[u % RING], 16 * loads)
                for t in range(TT):
                    ins = nc.tensor.transpose(MX[par][:, t * P:(t + 1) * P], C[u % RING][:, t, :], ident[:, :])
                ins.then_inc(kt_ready, 1)

            pe.wait_ge(aux_ready, 1)
            nc.tensor.transpose(SM[:, 0:P], aux[:, :], ident[:, :]).then_inc(aux_t, 1)
            keys_item(0, 0, BUFFER["keys", 0], 1)

            def transpose_x(b):
                pe.wait_ge(xn_ready, (b + 1) * ST)
                for k in range(KCH):
                    i = b * KCH + k
                    if i >= 2:
                        pe.wait_ge(y_ready, i - 1)
                    for t in range(ST):
                        ins = nc.tensor.transpose(SX[i % 2][:, t * P:(t + 1) * P], XS[:, b * ST + t, k * P:(k + 1) * P], ident[:, :])
                    ins.then_inc(xt_ready, 1)

            def project(g, b):
                pe.wait_ge(q_copied, 2 * g + b + 1)
                ops = [(WTh, XTh), (WTl, XTh), (WTh, XTl)]
                for k in range(KCH):
                    for o, (w, v) in enumerate(ops):
                        ins = nc.tensor.matmul(QP[b][:, :], w[g % 2][:, k * P:(k + 1) * P], v[b][:, k, :],
                                               start=(k == 0 and o == 0), stop=(k == KCH - 1 and o == 2))
                ins.then_inc(q_done, 1)

            transpose_x(0)
            wt_transposes(0)
            transpose_x(1)

            def max_item(n, u, i, par):
                h, st = divmod(i, ST)
                if st == 0:
                    pe.wait_ge(stack_in[h], 96 * (n + 1))
                for half in range(2):
                    cs = slice(half * 512, (half + 1) * 512)
                    ins = nc.tensor.matmul(MX[par][:, cs], QS[u % RING][0:BIAS, h, st * P:(st + 1) * P],
                                           KS[u % RING][0:BIAS, h, cs], start=True, stop=True)
                ins.then_inc(m_ready, 1)

            def bias_item(n, par):
                pe.wait_ge(mm_ready, 3 * (n + 1))
                for st in range(ST):
                    ins = nc.tensor.transpose(MX[par][:, st * P:(st + 1) * P], MM[:, st * 2 * HPG:st * 2 * HPG + P], ident[:, :])
                ins.then_inc(bt_ready, 1)

            def scores(n, u, tt, h):
                q = TT * HPG * n + HPG * tt + h
                if tt == 0:
                    pe.wait_ge(bias_in[h], 16 * (n + 1))
                pe.wait_ge(exp_done, q + 1)
                nc.tensor.matmul(SX[h % 2][:, :], KS[u % RING][0:ROWS, h, tt * P:(tt + 1) * P], QS[u % RING][0:ROWS, h, :],
                                 start=True, stop=True).then_inc(scores_ready, 1)

            def sum_probs(tile, start, stop):
                for h in range(HPG):
                    ins = nc.tensor.matmul(SM[h * HD:(h + 1) * HD, :], ones[:, :], tile(h), start=start, stop=stop,
                                           skip_group_check=True)
                return ins

            def values(n, u, tt):
                pe.wait_ge(exp_done, 2 + TT * HPG * n + HPG * (tt + 1))
                if tt == 0 and not is_first(n):
                    pe.wait_ge(pv_copied, n)
                for h in range(HPG):
                    ins = nc.tensor.matmul(PV[h * HD:(h + 1) * HD, :], C[u % RING][:, tt, h * HD:(h + 1) * HD],
                                           PR[:, tt % RING, h, :], start=(tt == 0), stop=(tt == TT - 1), skip_group_check=True)
                if tt == TT - 1:
                    ins.then_inc(pv_done, 1)
                if tt in POOL_TILES:
                    ins.then_inc(tile_used, 1)

            def direct_sum(n, tt):
                if tt not in POOL_TILES:
                    if tt == min(set(range(TT)) - set(POOL_TILES)):
                        if not is_first(n):
                            pe.wait_ge(sums_turned, n)
                        ins = sum_probs(lambda h: PR[:, tt % RING, h, :], True, False)
                    else:
                        ins = sum_probs(lambda h: PR[:, tt % RING, h, :], False, False)
                    ins.then_inc(tile_used, 1)

            def last_sum(n):
                pe.wait_ge(pool_used, ADDS * n + 2 * ADDS)
                sum_probs(lambda h: acc[:, h, :], False, True).then_inc(sums_done, 1)

            def before_step_0(at):
                kind, i = ORDER[at]
                old, o = ORDER[at - 2]
                if old == "wq":
                    pe.wait_ge(wt_lo, o + 1)
                elif old == "keys":
                    pe.wait_ge(mx_freed, 1)
                else:
                    pe.wait_ge(mx_freed, 1 + o + 1)
                if kind == "wq":
                    wt_transposes(i)
                elif kind == "max":
                    max_item(0, 0, i, at % 2)
                elif kind == "keys":
                    keys_item(i, i, at % 2, 1)
                else:
                    bias_item(0, at % 2)

            at = 2
            for g in range(GROUPS):
                end = at + len(WITH_GROUP[g])
                pe.wait_ge(wt_lo, g + 1)
                before_step_0(at)
                if g == GROUPS - 1:
                    at += 1
                    before_step_0(at)
                if g == 0:
                    pe.wait_ge(xt_split, KCH)
                project(g, 0)
                middle = (at + 1 + end + 1) // 2
                for i in range(at + 1, middle):
                    before_step_0(i)
                if g == 0:
                    pe.wait_ge(xt_split, BATCH * KCH)
                project(g, 1)
                for i in range(middle, end):
                    before_step_0(i)
                at = end
            pe.sem_inc(tile_used, RING)
            pe.wait_ge(onesrow_in, 16)

            def step(n, u, items, before, at, loads, freed, first=False):
                kinds = list(before)
                for tt in range(TT):
                    def mx_item(kind, a, i):
                        nonlocal at, freed
                        if kinds[-2] == "bias":
                            pe.wait_ge(bt_done, n + 1 + (len(kinds) >= 4))
                        else:
                            pe.wait_ge(mx_freed, freed - (kinds[-1] != "bias"))
                        if kind == "keys":
                            keys_item(n + a, u + a, at % 2, loads)
                        elif kind == "bias":
                            bias_item(n + a, at % 2)
                        else:
                            max_item(n + a, u + a, i, at % 2)
                        at += 1
                        freed = freed + (kind != "bias")
                        kinds.append(kind)

                    scores(n, u, tt, 0)
                    scores(n, u, tt, 1)
                    with_01, with_23 = items[tt]
                    if tt >= 1:
                        values(n, u, tt - 1)
                    elif not first:
                        values(n - 1, u + RING - 1, TT - 1)
                    for item in with_01:
                        mx_item(*item)
                    scores(n, u, tt, 2)
                    scores(n, u, tt, 3)
                    for item in with_23[:1]:
                        mx_item(*item)
                    if tt >= 1:
                        direct_sum(n, tt - 1)
                    elif not first:
                        direct_sum(n - 1, TT - 1)
                    if tt == SUM_SLOT and not first:
                        last_sum(n - 1)
                    for item in with_23[1:]:
                        mx_item(*item)

            last_kinds = [item[0] for item in ORDER[-2:]]
            step(0, 0, FIRST_STEP, last_kinds, FIRST_PARITY, 1, BEFORE, first=True)
            pe.wait_ge(onesrow_in, 16 * RING)
            last_kinds = [item[0] for item in flat(STEP)[-2:]]
            with pe.Fori(0, LOOPS) as j:
                for u in range(1, RING + 1):
                    n = RING * j + u
                    step(n, u, STEP, last_kinds, STEP_PARITY, j + 1 + (u + 2) // RING, vector_freed(n))
            for n in APART:
                step(n, n % RING, items_of(n), last_kinds, STEP_PARITY, (n + 2) // RING + 1, vector_freed(n))
            values(STEPS - 1, RING - 1, TT - 1)
            direct_sum(STEPS - 1, TT - 1)
            last_sum(STEPS - 1)

            pe.wait_ge(bt_done, STEPS)
            pe.wait_ge(mx_freed, vector_freed(STEPS - 2) + vector_items(items_of(STEPS - 2)))
            with pe.Fori(0, GROUPS // 2) as i:
                for par in range(2):
                    o = 2 * i + par
                    pe.wait_ge(wo_in[par], 16 * (i + 1))
                    pe.wait_ge(wo_lo, o + 1)
                    for k in range(KCH):
                        ins = nc.tensor.transpose(MX[par][:, k * P:(k + 1) * P], WS[par][:, k * P:(k + 1) * P], ident[:, :])
                    ins.then_inc(wo_ready, 1)
            pe.wait_ge(wo_lo, 2 + GROUPS)

            def project_out(t, q):
                pe.wait_ge(al_done, t + 1)
                for half in range(2):
                    cs = slice(half * 512, (half + 1) * 512)
                    ops = [(AH, WOh), (AL, WOh), (AH, WOl)]
                    for g in range(GROUPS):
                        for o, (a, w) in enumerate(ops):
                            ins = nc.tensor.matmul(MX[q][:, cs], a[q][:, g, :], w[:, g, cs],
                                                   start=(g == 0 and o == 0), stop=(g == GROUPS - 1 and o == 2))
                    ins.then_inc(o_ready, 1)

            with pe.Fori(0, TOK_TILES // 2) as i:
                for q in range(2):
                    project_out(2 * i + q, q)


_INS = ["x", "ctx_4096", "mask_BxS2_bf1", "L0_xattn_Wq", "L0_xattn_Wout", "L0_xattn_ln_gamma", "L0_xattn_ln_beta"]


def kernel(**inputs):
    import numpy as _np
    import concourse.bacc as _bacc
    from concourse import mybir as _mybir
    from concourse.bass_utils import run_bass_kernel_spmd as _run

    nc = _bacc.Bacc("TRN2", target_bir_lowering=False, num_devices=1)
    arrays, args = {}, []
    for name in _INS:
        a = _np.ascontiguousarray(inputs[name])
        if a.dtype == _np.bool_:
            a = a.view(_np.uint8)
        arrays[f"in_{name}"] = a
        args.append(nc.dram_tensor(f"in_{name}", a.shape, _mybir.dt.from_np(a.dtype), kind="ExternalInput").ap())
    out = nc.dram_tensor("out_0", (BATCH, S, HID), F32, kind="ExternalOutput").ap()
    build(nc, *args, out)
    r = _run(nc, [arrays], core_ids=[0])
    return r.results[0]["out_0"]
```

```python
import numpy as np
import concourse.bass as bass
from concourse import mybir

F32 = mybir.dt.float32
F32R = mybir.dt.float32r
BF16 = mybir.dt.bfloat16
U8 = mybir.dt.uint8
ALU = mybir.AluOpType
ACT = mybir.ActivationFunctionType

BATCH, S, HID = 2, 512, 1024
T = 1024
HD = 32
P = 128
HPG = P // HD
GROUPS = HID // P
STEPS = GROUPS * BATCH
TOK = BATCH * S
TOK_TILES = TOK // P
KCH = HID // P
TT = T // P
ST = S // P
RING = 4
BIAS = 3 * HD
ROWS = BIAS + 2
SCALE = float(HD) ** -0.5
EPS = 1e-5
BIG = 3.0e38
POOL_TILES = (0, 1, 2, 4, 5, 6)
ADDS = len(POOL_TILES) - 1
SUM_SLOT = 1
FIRST_DIRECT = min(set(range(TT)) - set(POOL_TILES))
DVE_T = 32
STACKED = 6 * 16
M_ITEMS = HPG * ST
WOUT_BLOCKS = HID // P
SUMS_AT = (2, 5, 7)
LAST_SUMS_AT = (2, 3, 4)
PROJECTED = [0, 2, 1, 3] + list(range(4, STEPS))


def keys(a):
    return [("keys", a, 0)]


def maxima(a, *items):
    return [("max", a, i) for i in items]


def wout(o):
    return [("wout", 0, o)]


def bias(a):
    return [("bias", a, 0)]


FIRST_STEP = [
    ([], []),
    ([], maxima(1, 0, 1)),
    (maxima(1, 2), maxima(1, 3, 4)),
    (maxima(1, 5), keys(2) + maxima(1, 6)),
    (maxima(1, 7), maxima(1, 8, 9)),
    (maxima(1, 10), maxima(1, 11, 12)),
    (maxima(1, 13), maxima(1, 14, 15)),
    (maxima(2, 0), bias(1) + maxima(2, 1, 2, 3)),
]
STEP = [
    ([], keys(2)),
    (maxima(1, 4), maxima(1, 5, 6)),
    ([], maxima(1, 7, 8)),
    ([], maxima(1, 9, 10)),
    (maxima(1, 11), maxima(1, 12, 13)),
    ([], maxima(1, 14, 15)),
    ([], maxima(2, 0) + bias(1)),
    (maxima(2, 1), maxima(2, 2, 3)),
]


def is_first(n):
    return isinstance(n, int) and n == 0


def items_of(n):
    items = [([i for i in with_01 if n + i[1] < STEPS], [i for i in with_23 if n + i[1] < STEPS])
             for with_01, with_23 in (FIRST_STEP if n == 0 else STEP)]
    if n == STEPS - 2:
        items[TT - 1] = (wout(0), wout(1))
    if n == STEPS - 1:
        items = [([], []) for _ in range(TT)]
        for o, tt in zip(range(2, WOUT_BLOCKS), (1, 2, 3, 5, 6, 7)):
            items[tt] = ([], wout(o))
    return items


def flat(items):
    return [i for slot in items for part in slot for i in part]


def vector_items(items):
    return sum(i[0] != "bias" for i in flat(items))


def with_group(g, first, count):
    return [("wq", g + 1)] + [("max", i) for i in range(first, first + count)]


WITH_GROUP = [with_group(0, 0, 0), with_group(1, 0, 2), with_group(2, 2, 4), with_group(3, 6, 3), with_group(4, 9, 3),
              with_group(5, 12, 3), with_group(6, 15, 1), [("bias", 0), ("keys", 1)]]
ORDER = [("wq", 0), ("keys", 0)] + [i for items in WITH_GROUP for i in items]
BUFFER = {item: at % 2 for at, item in enumerate(ORDER)}
FIRST_PARITY = len(ORDER) % 2
BEFORE = 2 + M_ITEMS
BEFORE_1 = BEFORE + vector_items(FIRST_STEP)
PER_STEP = vector_items(STEP)
STEP_PARITY = (FIRST_PARITY + len(flat(FIRST_STEP))) % 2


def vector_freed(n):
    return BEFORE_1 + PER_STEP * (n - 1)


VECTOR_FREED_LAST = vector_freed(STEPS - 2) + vector_items(items_of(STEPS - 2))
VECTOR_FREED_ALL = VECTOR_FREED_LAST + vector_items(items_of(STEPS - 1))
LAST_PARITY = (STEP_PARITY + len(flat(items_of(STEPS - 2)))) % 2


def build(nc, x, ctx, mask, wq, wout, gamma, beta, out):
    def sb(name, shape, dt):
        return nc.alloc_sbuf_tensor(name, shape, dt)

    ident = sb("ident", [P, P], F32)
    ones = sb("ones", [P, HD], F32)
    QA = sb("QA", [P, STEPS, S], F32)
    R = sb("R", [P, RING * HPG * (T + S)], F32R)
    KSZ, QSZ = HPG * T, HPG * S
    q_at = {2: RING * KSZ, 3: RING * KSZ + QSZ, 1: RING * KSZ + 2 * QSZ, 0: RING * KSZ + 3 * QSZ}
    KS = [R[:, r * KSZ:(r + 1) * KSZ].rearrange("p (h t) -> p h t", h=HPG) for r in range(RING)]
    QS = [R[:, q_at[r]:q_at[r] + QSZ].rearrange("p (h s) -> p h s", h=HPG) for r in range(RING)]
    XTh = [R[:, at:at + KCH * S].rearrange("p (k s) -> p k s", k=KCH) for at in (KSZ, 3 * KSZ)]
    XTl = [R[:, at:at + KCH * S].rearrange("p (k s) -> p k s", k=KCH) for at in (2 * KSZ, q_at[2])]
    KTh = sb("KTh", [P, T], F32R)
    KTl = sb("KTl", [P, T], F32R)
    WTh = [KTh[:, :], R[:, q_at[1]:q_at[1] + HID]]
    WTl = [KTl[:, :], R[:, q_at[1] + HID:q_at[1] + 2 * HID]]
    WOh = [R[:, at:at + GROUPS * S].rearrange("p (g n) -> p g n", n=S) for at in (0, 2 * KSZ)]
    WOl = [R[:, at:at + GROUPS * S].rearrange("p (g n) -> p g n", n=S) for at in (KSZ, q_at[1])]
    AH = [at.rearrange("p (g n) -> p g n", g=GROUPS) for at in (R[:, q_at[2]:q_at[2] + HID], KTh[:, :])]
    AL = [at.rearrange("p (g n) -> p g n", g=GROUPS) for at in (R[:, q_at[2] + HID:q_at[2] + 2 * HID], KTl[:, :])]
    C = [sb(f"C{r}", [P, TT, P], F32) for r in range(RING)]
    WR = [C[i][:, :, :].rearrange("p a c -> p (a c)") for i in range(2)]
    YT = [C[3][:, 4 * i:4 * i + 4, :].rearrange("p a c -> p (a c)") for i in range(2)]
    PR = sb("PR", [P, RING, HPG, S], F32)
    XS = PR[:, :, :, :].rearrange("p a b c -> p (a b c)").rearrange("p (t c) -> p t c", t=TOK_TILES)
    acc = sb("acc", [P, HPG, S], F32)
    WS = [acc[:, 2 * g:2 * g + 2, :].rearrange("p a b -> p (a b)") for g in range(2)]
    QTh = sb("QTh", [P, S], F32R)
    QTl = sb("QTl", [P, S], F32R)
    rsum = sb("rsum", [P, S], F32)
    rcol = sb("rcol", [P, S // DVE_T], F32)
    warm = sb("warm", [P, 1], F32)
    BT = sb("BT", [2 * HPG, S], F32R)
    maskadd = sb("maskadd", [P, BATCH, T], BF16)
    maskrow = rsum[:, :].bitcast(U8).rearrange("p (b t) -> p b t", b=BATCH)
    mx = sb("mx", [P, 2, M_ITEMS], F32)
    mxh = sb("mxh", [P, 2, M_ITEMS], F32R)
    MM = sb("MM", [P, (ST - 1) * 2 * HPG + P], F32)
    onesrow = QA[0:2, STEPS // 2:STEPS // 2 + 8, :]
    aux = sb("aux", [P, P], F32)
    auxm = sb("auxm", [P, P], U8)
    cols = sb("cols", [P, P], F32)
    stats = sb("stats", [P, TOK_TILES, 2, 6], F32)
    mv = sb("mv", [P, TOK_TILES, 2], F32)
    veps = sb("veps", [P, TOK_TILES], F32)
    sd = sb("sd", [P, TOK_TILES], F32)
    rstd = sb("rstd", [P, TOK_TILES], F32)
    newt = sb("newt", [P, TOK_TILES], F32)
    nmr = sb("nmr", [P, TOK_TILES], F32)
    GAM, BET, MSK = 0, 32, 64

    MX = [nc.alloc_psum_tensor(f"MX{i}", [P, T], F32) for i in range(2)]
    SX = [nc.alloc_psum_tensor(f"SX{i}", [P, S], F32) for i in range(2)]
    PV = nc.alloc_psum_tensor("PV", [P, S], F32)
    SM = nc.alloc_psum_tensor("SM", [P, S], F32)
    QP = [PV, SM]

    sem = nc.alloc_semaphore
    const_done = sem("const_done")
    aux_in, aux_ready, aux_t, cols_ready = sem("aux_in"), sem("aux_ready"), sem("aux_t"), sem("cols_ready")
    maskrow_in = sem("maskrow_in")
    onesrow_ready, onesrow_in = sem("onesrow_ready"), sem("onesrow_in")
    x_in = [sem(f"x_in{t}") for t in range(TOK_TILES)]
    chain = sem("chain")
    var_ready, sd_ready, norm_ready, xn_ready = sem("var_ready"), sem("sd_ready"), sem("norm_ready"), sem("xn_ready")
    xt_ready, y_ready, xt_split = sem("xt_ready"), sem("y_ready"), sem("xt_split")
    w_in = [sem(f"w_in{g}") for g in range(2)]
    wt_ready, wt_hi, wt_lo, q_done, q_copied = sem("wt_ready"), sem("wt_hi"), sem("wt_lo"), sem("q_done"), sem("q_copied")
    c_in = [sem(f"c_in{r}") for r in range(RING)]
    kt_ready, kt_hi, kt_lo, qt_hi, qt_lo = sem("kt_ready"), sem("kt_hi"), sem("kt_lo"), sem("qt_hi"), sem("qt_lo")
    stack_in = [sem(f"stack_in{h}") for h in range(HPG)]
    m_ready, mx_freed, mm_ready, bt_ready, bt_done = (
        sem("m_ready"), sem("mx_freed"), sem("mm_ready"), sem("bt_ready"), sem("bt_done"))
    bias_in = [sem(f"bias_in{h}") for h in range(HPG)]
    sums_turned, recip_ready = sem("sums_turned"), sem("recip_ready")
    scores_ready, exp_done, tile_used, pool_used = sem("scores_ready"), sem("exp_done"), sem("tile_used"), sem("pool_used")
    gate = sem("gate")
    pv_done, pv_copied, sums_done, rsum_done, attn_done = (
        sem("pv_done"), sem("pv_copied"), sem("sums_done"), sem("rsum_done"), sem("attn_done"))
    wo_in = [sem(f"wo_in{g}") for g in range(2)]
    wo_ready, wo_hi = sem("wo_ready"), sem("wo_hi")
    xr_in = [sem(f"xr_in{q}") for q in range(2)]
    ah_done, al_done, o_ready, o_added = sem("ah_done"), sem("al_done"), sem("o_ready"), sem("o_added")
    out_in = [sem(f"out_in{q}") for q in range(2)]

    ctx_v = ctx.rearrange("b (t p) (g c) -> p b t g c", p=P, c=P)
    xt_v = x.rearrange("b (t p) c -> p (b t) c", p=P)
    out_v = out.rearrange("b (t p) c -> p (b t) c", p=P)
    wq_v = wq.rearrange("(g p) c -> p g c", p=P)
    wo_v = wout.rearrange("(g p) c -> p g c", p=P)
    QAt = QA[:, :, :].rearrange("p (g b) s -> p g (b s)", b=BATCH)

    LOOPS = STEPS // RING - 1
    APART = range(LOOPS * RING + 1, STEPS)

    with nc.Block() as block:

        @block.sync
        def _(sp):
            def load_values(r, b, g):
                sp.dma_start(C[r][:, :, :], ctx_v[:, b, :, bass.ds(g, 1), :].rearrange("p t a c -> p t (a c)")).then_inc(c_in[r], 16)

            def load_wq(par, g):
                sp.dma_start(WS[par], wq_v[:, bass.ds(g, 1), :].rearrange("p a c -> p (a c)")).then_inc(w_in[par], 16)

            for t in range(ST):
                sp.dma_start(XS[:, t, :], xt_v[:, t, :]).then_inc(x_in[t], 16)
            load_values(0, 0, 0)
            load_wq(0, 0)
            for t in range(ST, TOK_TILES):
                sp.dma_start(XS[:, t, :], xt_v[:, t, :]).then_inc(x_in[t], 16)
            load_wq(1, 1)
            load_values(1, 1, 0)
            load_values(2, 0, 1)

            def key_rows(r, h):
                own = slice(h * HD, (h + 1) * HD)
                sp.dma_start(KS[r][0:HD, h, :].bitcast(F32), KTh[own, :].bitcast(F32)).then_inc(stack_in[h], 16)
                sp.dma_start(KS[r][HD:2 * HD, h, :].bitcast(F32), KTl[own, :].bitcast(F32)).then_inc(stack_in[h], 16)
                sp.dma_start(KS[r][2 * HD:3 * HD, h, :].bitcast(F32), KTh[own, :].bitcast(F32)).then_inc(stack_in[h], 16)

            def query_rows(r, h):
                own = slice(h * HD, (h + 1) * HD)
                sp.dma_start(QS[r][0:HD, h, :].bitcast(F32), QTh[own, :].bitcast(F32)).then_inc(stack_in[h], 16)
                sp.dma_start(QS[r][HD:2 * HD, h, :].bitcast(F32), QTh[own, :].bitcast(F32)).then_inc(stack_in[h], 16)
                sp.dma_start(QS[r][2 * HD:3 * HD, h, :].bitcast(F32), QTl[own, :].bitcast(F32)).then_inc(stack_in[h], 16)

            def keys_split(n):
                sp.wait_ge(kt_hi, n + 1)
                sp.wait_ge(kt_lo, n + 1)

            def queries_split(n):
                sp.wait_ge(qt_hi, n + 1)
                sp.wait_ge(qt_lo, n + 1)

            def stack(n, u):
                queries_split(n)
                keys_split(n)
                for h in range(HPG):
                    key_rows(u % RING, h)
                    query_rows(u % RING, h)

            def bias_rows(n, u):
                r = u % RING
                sp.wait_ge(bt_done, n + 1)
                for h in range(HPG):
                    sp.dma_start(QS[r][BIAS:ROWS, h, :].bitcast(F32), BT[2 * h:2 * h + 2, :].bitcast(F32)).then_inc(bias_in[h], 16)

            def next_wq(par, g):
                sp.wait_ge(wt_ready, g + 1)
                load_wq(par, g + 2)

            keys_split(0)
            for h in range(HPG):
                key_rows(0, h)
            sp.wait_ge(onesrow_ready, 1)
            sp.dma_start(KS[0][BIAS:ROWS, :, :].rearrange("p h t -> p (h t)").bitcast(F32),
                         onesrow.rearrange("p n s -> p (n s)")).then_inc(onesrow_in, 16)
            next_wq(0, 0)
            next_wq(1, 1)
            queries_split(0)
            for h in range(HPG):
                query_rows(0, h)
            with sp.Fori(1, GROUPS // 2 - 1) as i:
                for g in range(2):
                    next_wq(g, 2 * i + g)
            bias_rows(0, 0)
            sp.wait_ge(q_done, BATCH * GROUPS - 1)
            keys_split(1)
            for h in range(2):
                key_rows(1, h)
            queries_split(1)
            sp.wait_ge(q_done, BATCH * GROUPS)
            for h in range(2):
                query_rows(1, h)
            for h in range(2, HPG):
                key_rows(1, h)
                query_rows(1, h)
            sp.wait_ge(onesrow_in, 16)
            for r in range(1, RING):
                sp.dma_start(KS[r][BIAS:ROWS, :, :].bitcast(F32), KS[0][BIAS:ROWS, :, :].bitcast(F32)).then_inc(onesrow_in, 16)
            load_values(3, 1, 1)
            stack(2, 2)
            bias_rows(1, 1)

            def step(n, u, g, values, stacks, bias):
                if values:
                    sp.wait_ge(pv_done, n)
                    load_values((u + 3) % RING, (u + 3) % BATCH, g)
                if stacks:
                    stack(n + 2, u + 2)
                if bias:
                    bias_rows(n + 1, u + 1)

            with sp.Fori(0, LOOPS) as j:
                for u in range(1, RING + 1):
                    step(RING * j + u, u, 2 * j + (u + 3) // BATCH, True, True, True)
            for n in APART:
                if n == STEPS - 2:
                    for g in range(2):
                        sp.wait_ge(pv_done, n - 1 + g)
                        sp.dma_start(WR[g], wo_v[:, g, :]).then_inc(wo_in[g], 16)
                step(n, n % RING, (n + 3) // BATCH, n + 3 < STEPS, n + 2 < STEPS, n + 1 < STEPS)
            with sp.Fori(0, WOUT_BLOCKS // 2 - 1) as i:
                for g in range(2):
                    sp.wait_ge(wo_ready, 2 * i + g + 1)
                    sp.dma_start(WR[g], wo_v[:, bass.ds(2 * i + g + 2, 1), :].rearrange("p a c -> p (a c)")).then_inc(wo_in[g], 16)
            sp.wait_ge(sums_done, STEPS)
            for q in range(2):
                sp.dma_start(XS[:, q, :], xt_v[:, q, :]).then_inc(xr_in[q], 16)

            def store(t, q):
                sp.wait_ge(o_added, 2 * t + 2)
                sp.dma_start(out_v[:, bass.ds(t, 1), :].rearrange("p a c -> p (a c)"), XS[:, 2 + q, :]).then_inc(out_in[q], 16)

            with sp.Fori(0, TOK_TILES // 2 - 1) as i:
                for q in range(2):
                    t = 2 * i + q
                    store(t, q)
                    sp.dma_start(XS[:, q, :], xt_v[:, bass.ds(t + 2, 1), :].rearrange("p a c -> p (a c)")).then_inc(xr_in[q], 16)
            store(TOK_TILES - 2, 0)
            for half in range(2):
                cs = slice(half * S, (half + 1) * S)
                sp.wait_ge(o_added, 2 * TOK_TILES - 1 + half)
                sp.dma_start(out_v[:, TOK_TILES - 1, cs], XS[:, 3, cs]).then_inc(out_in[1], 16)
            sp.wait_ge(out_in[0], 16 * TOK_TILES // 2)
            sp.wait_ge(out_in[1], 16 * (TOK_TILES // 2 + 1))

        @block.gpsimd
        def _(pool):
            pool.sem_inc(attn_done, 1)
            nc.gpsimd.memset(aux[:, :], 0.0).then_inc(const_done, 1)
            nc.gpsimd.memset(ident[:, :], 0.0).then_inc(const_done, 1)
            nc.gpsimd.memset(ones[:, :], 1.0).then_inc(const_done, 1)
            pool.wait_ge(const_done, 3)
            nc.gpsimd.affine_select(out=ident[:, :], in_=ident[:, :], compare_op=ALU.not_equal, fill=1.0,
                                    base=0, pattern=[[-1, P]], channel_multiplier=1).then_inc(const_done, 1)
            pool.dma_start(maskrow, mask.rearrange("b t -> (b t)").partition_broadcast(P).rearrange("p (b t) -> p b t", b=BATCH)).then_inc(maskrow_in, 16)
            nc.gpsimd.memset(MM[:, :], 0.0).then_inc(const_done, 1)
            nc.gpsimd.memset(onesrow, 1.0).then_inc(onesrow_ready, 1)

            pool.sem_inc(pool_used, ADDS)

            def normalise(n):
                pool.wait_ge(pv_copied, n + 1)
                pool.wait_ge(rsum_done, n + 1)
                pool.sem_inc(gate, 1)
                at = QA[:, bass.ds(n, 1), :].rearrange("p a s -> p (a s)")
                nc.gpsimd.tensor_tensor(at, at, rsum[:, :], ALU.mult).then_inc(attn_done, 1)

            def add_probs(n, k):
                first, tt = POOL_TILES[0], POOL_TILES[k + 1]
                if k == 0:
                    if not is_first(n):
                        pool.wait_ge(sums_done, n)
                else:
                    pool.wait_ge(pool_used, ADDS * n + ADDS + k)
                pool.wait_ge(exp_done, 2 + TT * HPG * n + HPG * (tt + 1))
                a = PR[:, first % RING, :, :] if k == 0 else acc[:, :, :]
                nc.gpsimd.tensor_tensor(acc[:, :, :], a, PR[:, tt % RING, :, :], ALU.add).then_inc(pool_used, 1)

            def step(n, last=False):
                for k in range(ADDS):
                    add_probs(n, k)
                    if last and k == ADDS - 2:
                        normalise(n - 1)
                if not is_first(n) and not last:
                    normalise(n - 1)

            step(0)
            with pool.Fori(0, LOOPS) as j:
                for u in range(1, RING + 1):
                    step(RING * j + u)
            for n in APART:
                step(n, n == STEPS - 1)
            normalise(STEPS - 1)

        @block.scalar
        def _(act):
            act.wait_ge(const_done, 1)
            act.dma_start(aux[GAM:GAM + KCH, :], gamma.rearrange("(k p) -> k p", p=P)).then_inc(aux_in, 16)
            act.dma_start(aux[BET:BET + KCH, :], beta.rearrange("(k p) -> k p", p=P)).then_inc(aux_in, 16)
            act.dma_start(auxm[MSK:MSK + BATCH * TT, :], mask.rearrange("b (t p) -> (b t) p", p=P)).then_inc(aux_in, 16)

            def deviations(b):
                act.wait_ge(var_ready, b + 1)
                ts = slice(b * ST, (b + 1) * ST)
                nc.scalar.activation(sd[:, ts], veps[:, ts], ACT.Sqrt).then_inc(sd_ready, 1)

            def normalised(t):
                act.wait_ge(norm_ready, t // ST + 1)
                nc.scalar.activation(XS[:, t, :], XS[:, t, :], ACT.Identity, scale=rstd[:, t:t + 1],
                                     bias=nmr[:, t:t + 1]).then_inc(xn_ready, 1)

            def scaled(i):
                k = i % KCH
                act.wait_ge(xt_ready, i + 1)
                if i >= 2:
                    act.wait_ge(xt_split, i - 1)
                nc.scalar.activation(YT[i % 2], SX[i % 2][:, :], ACT.Identity, scale=cols[:, GAM + k:GAM + k + 1],
                                     bias=cols[:, BET + k:BET + k + 1]).then_inc(y_ready, 1)

            def key_high(n, par):
                act.wait_ge(kt_ready, n + 1)
                if not is_first(n):
                    for h in range(HPG):
                        act.wait_ge(stack_in[h], STACKED * n)
                nc.scalar.activation(KTh[:, :], MX[par][:, :], ACT.Copy).then_inc(kt_hi, 1)

            deviations(0)
            for t in range(ST):
                normalised(t)
            key_high(0, BUFFER["keys", 0])
            act.wait_ge(cols_ready, 1)
            scaled(0)
            deviations(1)
            for i in range(1, KCH):
                scaled(i)
                if i % 2:
                    normalised(ST + i // 2)

            def wt_high(g):
                act.wait_ge(wt_ready, g + 1)
                nc.scalar.activation(WTh[g % 2], MX[BUFFER["wq", g]][:, :], ACT.Copy).then_inc(wt_hi, 1)

            def q_copy(n, step_of):
                act.wait_ge(q_done, n + 1)
                nc.scalar.activation(QA[:, step_of, :], QP[step_of % BATCH][:, :], ACT.Copy).then_inc(q_copied, 1)

            def bias_copy(n, par):
                act.wait_ge(bt_ready, n + 1)
                if not is_first(n):
                    for h in range(HPG):
                        act.wait_ge(bias_in[h], 16 * n)
                nc.scalar.activation(BT[:, :], MX[par][0:2 * HPG, 0:S], ACT.Copy).then_inc(bt_done, 1)

            act.sem_inc(q_copied, 2)
            act.wait_ge(onesrow_in, 16)
            for h in range(HPG):
                act.wait_ge(stack_in[h], STACKED // 2)
            wt_high(0)
            scaled(KCH)
            scaled(KCH + 1)
            wt_high(1)
            for i in range(KCH + 2, 2 * KCH):
                scaled(i)
            for n, step_of in enumerate(PROJECTED[:2 * BATCH]):
                if n == 2 * BATCH - 1:
                    act.wait_ge(q_done, 2 * BATCH - 1)
                    wt_high(2)
                q_copy(n, step_of)
            for g in range(2, GROUPS):
                if g + 1 < GROUPS:
                    act.wait_ge(q_done, BATCH * g)
                    wt_high(g + 1)
                else:
                    bias_copy(0, BUFFER["bias", 0])
                    act.wait_ge(q_done, BATCH * g)
                    nc.scalar.activation(warm[:, :], cols[:, 0:1], ACT.Exp)
                    key_high(1, BUFFER["keys", 1])
                for b in range(BATCH):
                    q_copy(BATCH * g + b, BATCH * g + b)

            def exps(n, u, tt, pair):
                for h in (2 * pair, 2 * pair + 1):
                    q = TT * HPG * n + HPG * tt + h
                    if h == 0:
                        act.wait_ge(tile_used, TT * n + tt + 1)
                        old, m = (tt - RING, n) if tt >= RING else (tt + RING, n - 1)
                        if old in POOL_TILES:
                            act.wait_ge(pool_used, ADDS * m + ADDS + max(POOL_TILES.index(old), 1))
                    act.wait_ge(scores_ready, q + 1)
                    b = u % BATCH
                    nc.scalar.activation(PR[:, tt % RING, h, :], SX[h % 2][:, :], ACT.Exp, scale=SCALE,
                                         bias=cols[:, MSK + b * TT + tt:MSK + b * TT + tt + 1]).then_inc(exp_done, 1)

            act.sem_inc(exp_done, 2)

            def pv_copy(n):
                act.wait_ge(pv_done, n + 1)
                nc.scalar.activation(QA[:, bass.ds(n, 1), :].rearrange("p a s -> p (a s)"), PV[:, :], ACT.Copy).then_inc(pv_copied, 1)

            def high_and_bias(n, items, at):
                for kind, a, i in items:
                    if kind == "keys":
                        key_high(n + a, at % 2)
                    if kind == "bias":
                        bias_copy(n + a, at % 2)
                    at += 1
                return at

            def step(n, u, items, at, first=False):
                for tt in range(TT):
                    exps(n, u, tt, 0)
                    if tt == 0 and not first:
                        pv_copy(n - 1)
                    at = high_and_bias(n, items[tt][0], at)
                    exps(n, u, tt, 1)
                    at = high_and_bias(n, items[tt][1], at)

            step(0, 0, FIRST_STEP, FIRST_PARITY, first=True)
            with act.Fori(0, LOOPS) as j:
                for u in range(1, RING + 1):
                    step(RING * j + u, u, STEP, STEP_PARITY)
            for n in APART:
                step(n, n % RING, items_of(n), STEP_PARITY)
            pv_copy(STEPS - 1)

        @block.vector
        def _(dve):
            links = [0]

            def link(ins):
                links[0] += 1
                ins.then_inc(chain, 1)
                dve.wait_ge(chain, links[0])

            def statistics(b):
                ts = slice(b * ST, (b + 1) * ST)
                for t in range(b * ST, (b + 1) * ST):
                    dve.wait_ge(x_in[t], 16)
                    for half in range(2):
                        ins = nc.vector.bn_stats(stats[:, t, half, :], XS[:, t, half * S:(half + 1) * S])
                link(ins)
                for t in range(b * ST, (b + 1) * ST):
                    ins = nc.vector.bn_aggr(mv[:, t, :], stats[:, t, :, :].rearrange("p a b -> p (a b)"))
                link(ins)
                nc.vector.tensor_scalar(veps[:, ts], mv[:, ts, 1], EPS, None, ALU.add).then_inc(var_ready, 1)

            def norm_factors(b):
                ts = slice(b * ST, (b + 1) * ST)
                dve.wait_ge(sd_ready, b + 1)
                link(nc.vector.reciprocal(rstd[:, ts], sd[:, ts]))
                link(nc.vector.tensor_tensor(newt[:, ts], rstd[:, ts], rstd[:, ts], ALU.mult))
                link(nc.vector.tensor_tensor(newt[:, ts], newt[:, ts], veps[:, ts], ALU.mult))
                link(nc.vector.tensor_scalar(newt[:, ts], newt[:, ts], -0.5, 1.5, ALU.mult, ALU.add))
                link(nc.vector.tensor_tensor(rstd[:, ts], rstd[:, ts], newt[:, ts], ALU.mult))
                nc.vector.scalar_tensor_tensor(nmr[:, ts], mv[:, ts, 0], -1.0, rstd[:, ts], ALU.mult, ALU.mult).then_inc(norm_ready, 1)

            def split_x(i):
                b, k = divmod(i, KCH)
                dve.wait_ge(y_ready, i + 1)
                link(nc.vector.tensor_copy(XTh[b][:, k, :], YT[i % 2]))
                nc.vector.tensor_tensor(XTl[b][:, k, :], YT[i % 2], XTh[b][:, k, :].bitcast(F32), ALU.subtract).then_inc(xt_split, 1)

            def key_low(n, par):
                dve.wait_ge(kt_hi, n + 1)
                nc.vector.tensor_tensor(KTl[:, :], MX[par][:, :], KTh[:, :].bitcast(F32), ALU.subtract).then_inc(kt_lo, 1)
                dve.wait_ge(kt_lo, n + 1)
                dve.sem_inc(mx_freed, 1)

            def w_low(g):
                dve.wait_ge(wt_hi, g + 1)
                nc.vector.tensor_tensor(WTl[g % 2], MX[BUFFER["wq", g]][:, :], WTh[g % 2].bitcast(F32), ALU.subtract).then_inc(wt_lo, 1)

            statistics(0)
            norm_factors(0)
            dve.wait_ge(aux_in, 48)
            dve.wait_ge(const_done, 5)
            nc.vector.tensor_scalar(aux[MSK:MSK + BATCH * TT, :], auxm[MSK:MSK + BATCH * TT, :], BIG, -BIG,
                                    ALU.mult, ALU.add).then_inc(aux_ready, 1)
            dve.wait_ge(aux_t, 1)
            nc.vector.tensor_copy(cols[:, :], SM[:, 0:P]).then_inc(cols_ready, 1)
            statistics(1)
            key_low(0, BUFFER["keys", 0])
            norm_factors(1)
            for i in range(KCH):
                split_x(i)
            w_low(0)
            split_x(KCH)
            split_x(KCH + 1)
            w_low(1)
            for i in range(KCH + 2, 2 * KCH):
                split_x(i)
            dve.wait_ge(maskrow_in, 16)
            for b in range(BATCH):
                ins = nc.vector.tensor_scalar(maskadd[:, b, :], maskrow[:, b, :], BIG, -BIG, ALU.mult, ALU.add)
            link(ins)

            def split_queries(n):
                if not is_first(n):
                    for h in range(HPG):
                        dve.wait_ge(stack_in[h], STACKED * n)
                q = QA[:, bass.ds(n, 1), :].rearrange("p a s -> p (a s)")
                nc.vector.tensor_copy(QTh[:, :], q).then_inc(qt_hi, 1)
                dve.wait_ge(qt_hi, n + 1)
                nc.vector.tensor_tensor(QTl[:, :], q, QTh[:, :].bitcast(F32), ALU.subtract).then_inc(qt_lo, 1)

            def maximum(n, u, i, par):
                h, st = divmod(i, ST)
                c = st * HPG + h
                dve.wait_ge(m_ready, M_ITEMS * n + i + 1)
                dve.sem_inc(gate, 1)
                nc.vector.tensor_tensor_reduce(out=MX[par][:, :], in0=MX[par][:, :], in1=maskadd[:, u % BATCH, :], scale=1.0,
                                               scalar=-BIG, op0=ALU.add, op1=ALU.max,
                                               accum_out=mx[:, u % 2, c:c + 1]).then_inc(mx_freed, 1)

            def bias_columns(n, u, freed):
                dve.wait_ge(mx_freed, freed)
                if not is_first(n):
                    dve.wait_ge(bt_ready, n)
                nc.vector.tensor_scalar(mxh[:, u % 2, :], mx[:, u % 2, :], -1.0, None, ALU.mult).then_inc(mm_ready, 1)
                dve.wait_ge(mm_ready, 3 * n + 1)
                hi = mxh[:, u % 2, :].bitcast(F32)
                cols_of = MM[:, 0:ST * 2 * HPG].rearrange("p (s h a) -> p s h a", h=HPG, a=2)
                nc.vector.tensor_copy(cols_of[:, :, :, 0], hi.rearrange("p (s h) -> p s h", h=HPG)).then_inc(mm_ready, 1)
                nc.vector.scalar_tensor_tensor(cols_of[:, :, :, 1], mx[:, u % 2, :].rearrange("p (s h) -> p s h", h=HPG), -1.0,
                                               hi.rearrange("p (s h) -> p s h", h=HPG), ALU.mult, ALU.subtract).then_inc(mm_ready, 1)

            def invert_sums(n, part):
                if part == 0:
                    dve.wait_ge(sums_done, n + 1)
                    dve.wait_ge(attn_done, 1 + n)
                    nc.vector.transpose(rsum[:, :], SM[:, :]).then_inc(sums_turned, 1)
                if part == 1:
                    dve.wait_ge(sums_turned, n + 1)
                    nc.vector.reciprocal(rcol[:, :], rsum[:, :].rearrange("p (b i) -> p b i", i=DVE_T)[:, :, 0]).then_inc(recip_ready, 1)
                if part == 2:
                    dve.wait_ge(recip_ready, n + 1)
                    nc.vector.transpose(rsum[:, :].rearrange("p (b i) -> p b i", i=DVE_T),
                                        rcol[:, :].unsqueeze(2).to_broadcast([P, S // DVE_T, DVE_T])).then_inc(rsum_done, 1)

            dve.wait_ge(q_copied, 2 + 1)
            split_queries(0)
            for g in range(1, GROUPS):
                for item in WITH_GROUP[g]:
                    if item[0] == "wq":
                        w_low(item[1])
                    if item[0] == "max":
                        maximum(0, 0, item[1], BUFFER[item])
                if g == GROUPS - 4:
                    split_queries(1)
            bias_columns(0, 0, BEFORE - 1)
            key_low(1, BUFFER["keys", 1])

            def wout_parts(o, par):
                half, n = divmod(o * P, S)
                src = MX[par][:, :].rearrange("p (g n) -> p g n", n=P)
                dve.wait_ge(wo_ready, o + 1)
                nc.vector.tensor_copy(WOh[half][:, :, n:n + P], src).then_inc(wo_hi, 1)
                dve.wait_ge(wo_hi, o + 1)
                nc.vector.tensor_tensor(WOl[half][:, :, n:n + P], src, WOh[half][:, :, n:n + P].bitcast(F32),
                                        ALU.subtract).then_inc(mx_freed, 1)

            def step(n, u, items, at, freed, sums_at=SUMS_AT, first=False):
                for tt in range(TT):
                    if tt in sums_at and not first:
                        invert_sums(n - 1, sums_at.index(tt))
                    for kind, a, i in items[tt][0] + items[tt][1]:
                        if kind == "keys":
                            if a == 2:
                                split_queries(n + a)
                            key_low(n + a, at % 2)
                            freed = freed + 1
                        if kind == "wout":
                            wout_parts(i, at % 2)
                        if kind == "max":
                            maximum(n + a, u + a, i, at % 2)
                            freed = freed + 1
                            if i == M_ITEMS - 1:
                                bias_columns(n + a, u + a, freed)
                        at += 1

            step(0, 0, FIRST_STEP, FIRST_PARITY, BEFORE, first=True)
            with dve.Fori(0, LOOPS) as j:
                for u in range(1, RING + 1):
                    n = RING * j + u
                    step(n, u, STEP, STEP_PARITY, vector_freed(n))
            for n in APART[:-1]:
                step(n, n % RING, items_of(n), STEP_PARITY, vector_freed(n))
            n = STEPS - 1
            step(n, n % RING, items_of(n), LAST_PARITY, VECTOR_FREED_LAST, LAST_SUMS_AT)

            def split_attn(t, q):
                src = QAt[:, :, bass.ds(t * P, P)]
                nc.vector.tensor_copy(AH[q][:, :, :], src).then_inc(ah_done, 1)
                dve.wait_ge(ah_done, t + 1)
                nc.vector.tensor_tensor(AL[q][:, :, :], src, AH[q][:, :, :].bitcast(F32), ALU.subtract).then_inc(al_done, 1)

            def add_residual(t, i, q, stored=True):
                dve.wait_ge(xr_in[q], 16 * (i + 1))
                if stored:
                    dve.wait_ge(out_in[q], 16 * i)
                for half in range(2):
                    dve.wait_ge(o_ready, 2 * t + half + 1)
                    cs = slice(half * S, (half + 1) * S)
                    nc.vector.tensor_tensor(XS[:, 2 + q, cs], XS[:, q, cs], MX[q][:, cs], ALU.add).then_inc(o_added, 1)

            dve.wait_ge(attn_done, STEPS)
            split_attn(0, 0)
            split_attn(1, 1)
            for part in range(3):
                invert_sums(STEPS - 1, part)
            for q in range(2):
                add_residual(q, 0, q, stored=False)
                split_attn(q + 2, q)
            dve.wait_ge(attn_done, 1 + STEPS)
            with dve.Fori(1, TOK_TILES // 2 - 1) as i:
                for q in range(2):
                    add_residual(2 * i + q, i, q)
                    split_attn(2 * i + q + 2, q)
            for q in range(2):
                add_residual(TOK_TILES - 2 + q, TOK_TILES // 2 - 1, q)

        @block.tensor
        def _(pe):
            pe.wait_ge(const_done, 5)

            def wt_transposes(g):
                pe.wait_ge(w_in[g % 2], 16 * (g // 2 + 1))
                for k in range(KCH):
                    ins = nc.tensor.transpose(MX[BUFFER["wq", g]][:, k * P:(k + 1) * P], WS[g % 2][:, k * P:(k + 1) * P], ident[:, :])
                ins.then_inc(wt_ready, 1)

            def keys_item(n, u, par, loads):
                pe.wait_ge(c_in[u % RING], 16 * loads)
                for t in range(TT):
                    ins = nc.tensor.transpose(MX[par][:, t * P:(t + 1) * P], C[u % RING][:, t, :], ident[:, :])
                ins.then_inc(kt_ready, 1)

            pe.wait_ge(aux_ready, 1)
            nc.tensor.transpose(SM[:, 0:P], aux[:, :], ident[:, :]).then_inc(aux_t, 1)
            keys_item(0, 0, BUFFER["keys", 0], 1)

            def transpose_x(i):
                b, k = divmod(i, KCH)
                pe.wait_ge(xn_ready, (b + 1) * ST)
                if i >= 2:
                    pe.wait_ge(y_ready, i - 1)
                for t in range(ST):
                    ins = nc.tensor.transpose(SX[i % 2][:, t * P:(t + 1) * P], XS[:, b * ST + t, k * P:(k + 1) * P], ident[:, :])
                ins.then_inc(xt_ready, 1)

            def project(g, b, chunks=range(KCH)):
                ops = [(WTh, XTh), (WTl, XTh), (WTh, XTl)]
                for k in chunks:
                    for o, (w, v) in enumerate(ops):
                        ins = nc.tensor.matmul(QP[b][:, :], w[g % 2][:, k * P:(k + 1) * P], v[b][:, k, :],
                                               start=(k == 0 and o == 0), stop=(k == KCH - 1 and o == 2))
                if KCH - 1 in chunks:
                    ins.then_inc(q_done, 1)

            wt_transposes(0)
            for i in range(KCH + 2):
                transpose_x(i)
            pe.wait_ge(wt_lo, 1)
            wt_transposes(1)
            pe.wait_ge(xt_split, KCH)
            for k in range(KCH):
                if k >= 2:
                    transpose_x(KCH + k)
                project(0, 0, [k])
            pe.wait_ge(wt_lo, 2)
            pe.wait_ge(q_copied, 2 + 1)
            project(1, 0)
            pe.wait_ge(xt_split, BATCH * KCH)
            project(0, 1)

            def max_item(n, u, i, par):
                h, st = divmod(i, ST)
                if st == 0:
                    pe.wait_ge(stack_in[h], STACKED * (n + 1))
                for half in range(2):
                    cs = slice(half * S, (half + 1) * S)
                    ins = nc.tensor.matmul(MX[par][:, cs], QS[u % RING][0:BIAS, h, st * P:(st + 1) * P],
                                           KS[u % RING][0:BIAS, h, cs], start=True, stop=True)
                ins.then_inc(m_ready, 1)

            def bias_item(n, par):
                pe.wait_ge(mm_ready, 3 * (n + 1))
                for st in range(ST):
                    ins = nc.tensor.transpose(MX[par][:, st * P:(st + 1) * P], MM[:, st * 2 * HPG:st * 2 * HPG + P], ident[:, :])
                ins.then_inc(bt_ready, 1)

            def wout_item(o, par):
                pe.wait_ge(wo_in[o % 2], 16 * (o // 2 + 1))
                for k in range(KCH):
                    ins = nc.tensor.transpose(MX[par][:, k * P:(k + 1) * P], WR[o % 2][:, k * P:(k + 1) * P], ident[:, :])
                ins.then_inc(wo_ready, 1)

            def scores(n, u, tt, h):
                q = TT * HPG * n + HPG * tt + h
                if tt == 0:
                    pe.wait_ge(bias_in[h], 16 * (n + 1))
                pe.wait_ge(exp_done, q + 1)
                nc.tensor.matmul(SX[h % 2][:, :], KS[u % RING][0:ROWS, h, tt * P:(tt + 1) * P], QS[u % RING][0:ROWS, h, :],
                                 start=True, stop=True).then_inc(scores_ready, 1)

            def sum_probs(tile, start, stop):
                for h in range(HPG):
                    ins = nc.tensor.matmul(SM[h * HD:(h + 1) * HD, :], ones[:, :], tile(h), start=start, stop=stop,
                                           skip_group_check=True)
                return ins

            def values(n, u, tt):
                pe.wait_ge(exp_done, 2 + TT * HPG * n + HPG * (tt + 1))
                if tt == 0 and not is_first(n):
                    pe.wait_ge(pv_copied, n)
                for h in range(HPG):
                    ins = nc.tensor.matmul(PV[h * HD:(h + 1) * HD, :], C[u % RING][:, tt, h * HD:(h + 1) * HD],
                                           PR[:, tt % RING, h, :], start=(tt == 0), stop=(tt == TT - 1), skip_group_check=True)
                if tt == TT - 1:
                    ins.then_inc(pv_done, 1)
                if tt in POOL_TILES:
                    ins.then_inc(tile_used, 1)

            def direct_sum(n, tt):
                if tt not in POOL_TILES:
                    if tt == FIRST_DIRECT:
                        if not is_first(n):
                            pe.wait_ge(sums_turned, n)
                        ins = sum_probs(lambda h: PR[:, tt % RING, h, :], True, False)
                    else:
                        ins = sum_probs(lambda h: PR[:, tt % RING, h, :], False, False)
                    ins.then_inc(tile_used, 1)

            def last_sum(n):
                pe.wait_ge(pool_used, ADDS * n + 2 * ADDS)
                sum_probs(lambda h: acc[:, h, :], False, True).then_inc(sums_done, 1)

            def before_step_0(at):
                kind, i = ORDER[at]
                old, o = ORDER[at - 2]
                if old == "wq":
                    pe.wait_ge(wt_lo, o + 1)
                elif old == "keys":
                    pe.wait_ge(mx_freed, 1)
                else:
                    pe.wait_ge(mx_freed, 1 + o + 1)
                if kind == "wq":
                    wt_transposes(i)
                elif kind == "max":
                    max_item(0, 0, i, at % 2)
                elif kind == "keys":
                    keys_item(i, i, at % 2, 1)
                else:
                    bias_item(0, at % 2)

            at = 2 + len(WITH_GROUP[0])
            for g in range(1, GROUPS):
                end = at + len(WITH_GROUP[g])
                pe.wait_ge(wt_lo, g + 1)
                before_step_0(at)
                if g == GROUPS - 1:
                    at += 1
                    before_step_0(at)
                if g > 1:
                    pe.wait_ge(q_copied, 2 * g + 1)
                    project(g, 0)
                middle = (at + 1 + end + 1) // 2
                for i in range(at + 1, middle):
                    before_step_0(i)
                pe.wait_ge(q_copied, 2 * g + 2 if g > 1 else 2 * g + 3)
                project(g, 1)
                for i in range(middle, end):
                    before_step_0(i)
                at = end
            pe.sem_inc(tile_used, RING)
            pe.wait_ge(onesrow_in, 16)

            def step(n, u, items, before, at, loads, freed, first=False):
                kinds = list(before)
                for tt in range(TT):
                    def mx_item(kind, a, i):
                        nonlocal at, freed
                        if kinds[-2] == "bias":
                            pe.wait_ge(bt_done, n + 1 + (len(kinds) >= 4))
                        else:
                            pe.wait_ge(mx_freed, freed - (kinds[-1] != "bias"))
                        if kind == "keys":
                            keys_item(n + a, u + a, at % 2, loads)
                        elif kind == "bias":
                            bias_item(n + a, at % 2)
                        elif kind == "wout":
                            wout_item(i, at % 2)
                        else:
                            max_item(n + a, u + a, i, at % 2)
                        at += 1
                        freed = freed + (kind != "bias")
                        kinds.append(kind)

                    scores(n, u, tt, 0)
                    scores(n, u, tt, 1)
                    with_01, with_23 = items[tt]
                    if tt >= 1:
                        values(n, u, tt - 1)
                    elif not first:
                        values(n - 1, u + RING - 1, TT - 1)
                    for item in with_01:
                        mx_item(*item)
                    scores(n, u, tt, 2)
                    scores(n, u, tt, 3)
                    for item in with_23[:1]:
                        mx_item(*item)
                    if tt >= 1:
                        direct_sum(n, tt - 1)
                    elif not first:
                        direct_sum(n - 1, TT - 1)
                    if tt == SUM_SLOT and not first:
                        last_sum(n - 1)
                    for item in with_23[1:]:
                        mx_item(*item)

            last_kinds = [item[0] for item in ORDER[-2:]]
            step(0, 0, FIRST_STEP, last_kinds, FIRST_PARITY, 1, BEFORE, first=True)
            pe.wait_ge(onesrow_in, 16 * RING)
            last_kinds = [item[0] for item in flat(STEP)[-2:]]
            with pe.Fori(0, LOOPS) as j:
                for u in range(1, RING + 1):
                    n = RING * j + u
                    step(n, u, STEP, last_kinds, STEP_PARITY, j + 1 + (u + 2) // RING, vector_freed(n))
            for n in APART[:-1]:
                step(n, n % RING, items_of(n), last_kinds, STEP_PARITY, (n + 2) // RING + 1, vector_freed(n))
            n = STEPS - 1
            last_kinds = [item[0] for item in flat(items_of(n - 1))[-2:]]
            step(n, n % RING, items_of(n), last_kinds, LAST_PARITY, None, VECTOR_FREED_LAST)
            values(n, n % RING, TT - 1)
            direct_sum(n, TT - 1)

            def project_out(q, half):
                cs = slice(half * S, (half + 1) * S)
                ops = [(AH, WOh), (AL, WOh), (AH, WOl)]
                for g in range(GROUPS):
                    for o, (a, w) in enumerate(ops):
                        ins = nc.tensor.matmul(MX[q][:, cs], a[q][:, g, :], w[half][:, g, :],
                                               start=(g == 0 and o == 0), stop=(g == GROUPS - 1 and o == 2))
                ins.then_inc(o_ready, 1)

            pe.wait_ge(mx_freed, VECTOR_FREED_ALL - 1)
            pe.wait_ge(al_done, 1)
            project_out(0, 0)
            last_sum(STEPS - 1)
            pe.wait_ge(mx_freed, VECTOR_FREED_ALL)
            project_out(0, 1)
            pe.wait_ge(al_done, 2)
            project_out(1, 0)
            project_out(1, 1)
            with pe.Fori(1, TOK_TILES // 2) as i:
                for q in range(2):
                    pe.wait_ge(al_done, 2 * i + q + 1)
                    project_out(q, 0)
                    project_out(q, 1)


_INS = ["x", "ctx_4096", "mask_BxS2_bf1", "L0_xattn_Wq", "L0_xattn_Wout", "L0_xattn_ln_gamma", "L0_xattn_ln_beta"]


def kernel(**inputs):
    import numpy as _np
    import concourse.bacc as _bacc
    from concourse import mybir as _mybir
    from concourse.bass_utils import run_bass_kernel_spmd as _run

    nc = _bacc.Bacc("TRN2", target_bir_lowering=False, num_devices=1)
    arrays, args = {}, []
    for name in _INS:
        a = _np.ascontiguousarray(inputs[name])
        if a.dtype == _np.bool_:
            a = a.view(_np.uint8)
        arrays[f"in_{name}"] = a
        args.append(nc.dram_tensor(f"in_{name}", a.shape, _mybir.dt.from_np(a.dtype), kind="ExternalInput").ap())
    out = nc.dram_tensor("out_0", (BATCH, S, HID), F32, kind="ExternalOutput").ap()
    build(nc, *args, out)
    r = _run(nc, [arrays], core_ids=[0])
    return r.results[0]["out_0"]
```
